# Optimizing a Trainium2 kernel written in Bass

```python
import numpy as np
import jax
import jax.numpy as jnp

def _softmax(x, axis=-1):
    return jax.nn.softmax(x, axis=axis)

def _gelu(x):
    return jax.nn.gelu(x, approximate=True)

def _silu(x):
    return jax.nn.silu(x)

def _sigmoid(x):
    return jax.nn.sigmoid(x)

def _layernorm(x, axis=-1, eps=1e-05):
    m = jnp.mean(x, axis=axis, keepdims=True)
    v = jnp.var(x, axis=axis, keepdims=True)
    return (x - m) / jnp.sqrt(v + eps)

def _scatter_add(tgt, idx, src, axis=0):
    return tgt.at[idx].add(src)

def _segment_sum(src, seg, n):
    return jax.ops.segment_sum(src, seg, n)
kernel_name = 'mk_early_fusion_d1_tok_img1024_r4_94a5b7'

def setup_inputs(seed: int=0):
    np.random.seed(seed)
    _w = jnp.asarray

    def _rec_inputs():
        import jax
        import jax.numpy as jnp
        _rk = jax.random.key(seed)
        x = -0.00016672 + 0.999947 * jax.random.normal(jax.random.fold_in(_rk, 1), (64, 3, 96, 96), jnp.float32)
        txt = 0.00180885 + 1.15405 * jax.random.normal(jax.random.fold_in(_rk, 2), (64, 77, 256), jnp.float32)
        return (x, txt)
    x, txt = _rec_inputs()

    def _L0_tok_setup():
        import jax, jax.numpy as jnp
        import numpy as np
        PATCH = 16

        def _patchify(x, p):
            B, C, H, W = x.shape
            nh, nw = (H // p, W // p)
            x = x.reshape(B, C, nh, p, nw, p)
            x = x.transpose(0, 2, 4, 1, 3, 5)
            return x.reshape(B, nh * nw, C * p * p)
        key = jax.random.key(seed)
        k1, k2, k3, k4, k5 = jax.random.split(key, 5)
        B, C, H = (64, 3, 96)
        d_model = 256
        p = PATCH
        num_patches = (H // p) ** 2
        in_dim = p * p * C
        x = jax.random.normal(k1, (B, C, H, H), dtype=jnp.float32)
        bound = 1.0 / np.sqrt(in_dim)
        W = jax.random.uniform(k2, (d_model, in_dim), dtype=jnp.float32, minval=-bound, maxval=bound)
        b = jax.random.uniform(k3, (d_model,), dtype=jnp.float32, minval=-bound, maxval=bound)
        cls_token = jax.random.normal(k4, (1, 1, d_model), dtype=jnp.float32)
        pos_enc = jax.random.normal(k5, (1, num_patches + 1, d_model), dtype=jnp.float32)
        return {'x': x, 'W': W, 'b': b, 'cls_token': cls_token, 'pos_enc': pos_enc}
    _L0_tok_all = _L0_tok_setup()
    _L0_tok_in = {k: v for k, v in _L0_tok_all.items() if k in ('W', 'b', 'cls_token', 'pos_enc')}
    del _L0_tok_all

    def _L0_attn_setup():
        import jax, jax.numpy as jnp
        import numpy as np
        B, S, E, H = (4, 1024, 256, 16)
        D = E // H

        def _xavier(key, out_f, in_f):
            lim = float(np.sqrt(6.0 / (in_f + out_f)))
            return jax.random.uniform(key, (out_f, in_f), jnp.float32, -lim, lim)

        def _feature_map(t):
            return jax.nn.elu(t) + 1.0
        key = jax.random.key(seed)
        ks = jax.random.split(key, 9)
        x = jax.random.normal(ks[0], (B, S, E), jnp.float32)
        Wq = _xavier(ks[1], E, E)
        Wk = _xavier(ks[2], E, E)
        Wv = _xavier(ks[3], E, E)
        Wo = _xavier(ks[4], E, E)
        bq = jnp.zeros((E,), jnp.float32)
        bk = jnp.zeros((E,), jnp.float32)
        bv = jnp.zeros((E,), jnp.float32)
        bo = jnp.zeros((E,), jnp.float32)
        return {'x': x, 'Wq': Wq, 'bq': bq, 'Wk': Wk, 'bk': bk, 'Wv': Wv, 'bv': bv, 'Wo': Wo, 'bo': bo}
    _L0_attn_all = _L0_attn_setup()
    _L0_attn_in = {k: v for k, v in _L0_attn_all.items() if k in ('Wq', 'bq', 'Wk', 'bk', 'Wv', 'bv', 'Wo', 'bo')}
    del _L0_attn_all

    def _L0_ffn_setup():
        import jax, jax.numpy as jnp
        import numpy as np
        B, S, H, I, E = (2, 1024, 256, 128, 8)
        key = jax.random.key(seed)
        ks = jax.random.split(key, 5)
        scale_h = 1.0 / np.sqrt(H)
        scale_i = 1.0 / np.sqrt(I)
        return {'hidden_states': jax.random.normal(ks[0], (B, S, H), dtype=jnp.float32), 'gate_w': jax.random.normal(ks[1], (E, H), dtype=jnp.float32) * scale_h, 'w_gate': jax.random.normal(ks[2], (E, I, H), dtype=jnp.float32) * scale_h, 'w_up': jax.random.normal(ks[3], (E, I, H), dtype=jnp.float32) * scale_h, 'w_down': jax.random.normal(ks[4], (E, H, I), dtype=jnp.float32) * scale_i}
    _L0_ffn_all = _L0_ffn_setup()
    _L0_ffn_in = {k: v for k, v in _L0_ffn_all.items() if k in ('gate_w', 'w_gate', 'w_up', 'w_down')}
    del _L0_ffn_all
    return {'x': x, 'txt': txt, 'L0_tok_W': _L0_tok_in['W'], 'L0_tok_b': _L0_tok_in['b'], 'L0_tok_cls_token': _L0_tok_in['cls_token'], 'L0_tok_pos_enc': _L0_tok_in['pos_enc'], 'L0_attn_Wq': _L0_attn_in['Wq'], 'L0_attn_bq': _L0_attn_in['bq'], 'L0_attn_Wk': _L0_attn_in['Wk'], 'L0_attn_bk': _L0_attn_in['bk'], 'L0_attn_Wv': _L0_attn_in['Wv'], 'L0_attn_bv': _L0_attn_in['bv'], 'L0_attn_Wo': _L0_attn_in['Wo'], 'L0_attn_bo': _L0_attn_in['bo'], 'L0_ffn_gate_w': _L0_ffn_in['gate_w'], 'L0_ffn_w_gate': _L0_ffn_in['w_gate'], 'L0_ffn_w_up': _L0_ffn_in['w_up'], 'L0_ffn_w_down': _L0_ffn_in['w_down']}

def reference(x, txt, L0_tok_W, L0_tok_b, L0_tok_cls_token, L0_tok_pos_enc, L0_attn_Wq, L0_attn_bq, L0_attn_Wk, L0_attn_bk, L0_attn_Wv, L0_attn_bv, L0_attn_Wo, L0_attn_bo, L0_ffn_gate_w, L0_ffn_w_gate, L0_ffn_w_up, L0_ffn_w_down):
    import jax
    import jax.numpy as jnp

    def _L0_tok_ref(x, W, b, cls_token, pos_enc):
        import jax, jax.numpy as jnp
        import numpy as np
        PATCH = 16

        def _patchify(x, p):
            B, C, H, W = x.shape
            nh, nw = (H // p, W // p)
            x = x.reshape(B, C, nh, p, nw, p)
            x = x.transpose(0, 2, 4, 1, 3, 5)
            return x.reshape(B, nh * nw, C * p * p)
        B = x.shape[0]
        patches = _patchify(x, PATCH)
        proj = jnp.einsum('bnf,df->bnd', patches, W) + b
        cls = jnp.broadcast_to(cls_token, (B, 1, cls_token.shape[-1]))
        out = jnp.concatenate([cls, proj], axis=1) + pos_enc
        return out

    def _L0_attn_ref(x, Wq, bq, Wk, bk, Wv, bv, Wo, bo):
        import jax, jax.numpy as jnp
        import numpy as np
        B, S, E, H = (4, 1024, 256, 16)
        D = E // H

        def _xavier(key, out_f, in_f):
            lim = float(np.sqrt(6.0 / (in_f + out_f)))
            return jax.random.uniform(key, (out_f, in_f), jnp.float32, -lim, lim)

        def _feature_map(t):
            return jax.nn.elu(t) + 1.0
        b, s, _ = x.shape
        Q = (x @ Wq.T + bq).reshape(b, s, H, D)
        K = (x @ Wk.T + bk).reshape(b, s, H, D)
        V = (x @ Wv.T + bv).reshape(b, s, H, D)
        Q = _feature_map(Q)
        K = _feature_map(K)
        KV = jnp.einsum('bshd,bshe->bhde', K, V)
        K_sum = K.sum(axis=1)
        Z = 1.0 / (jnp.einsum('bshd,bhd->bsh', Q, K_sum) + 1e-06)
        out = jnp.einsum('bshd,bhde,bsh->bshe', Q, KV, Z)
        out = out.reshape(b, s, E)
        out = out @ Wo.T + bo
        return out

    def _L0_ffn_ref(hidden_states, gate_w, w_gate, w_up, w_down):
        import jax, jax.numpy as jnp
        import numpy as np
        B, S, H, I, E = (2, 1024, 256, 128, 8)
        b, s, h = hidden_states.shape
        x = hidden_states.reshape(-1, h)
        logits = x @ gate_w.T
        top_v = jnp.max(logits, axis=-1)
        sel = jnp.argmax(logits, axis=-1)
        rw = jax.nn.sigmoid(top_v)
        out = jnp.zeros_like(x)
        n_exp = gate_w.shape[0]
        for e in range(n_exp):
            mask = (sel == e).astype(x.dtype)
            xs = x * (rw * mask)[:, None]
            g = xs @ w_gate[e].T
            u = xs @ w_up[e].T
            out = out + u * jax.nn.silu(g) @ w_down[e].T
        return out.reshape(b, s, h)
    h = _L0_tok_ref(x, L0_tok_W, L0_tok_b, L0_tok_cls_token, L0_tok_pos_enc)
    h = jnp.concatenate([h, txt], axis=1)
    h = h + _L0_attn_ref(_layernorm(h, axis=-1), L0_attn_Wq, L0_attn_bq, L0_attn_Wk, L0_attn_bk, L0_attn_Wv, L0_attn_bv, L0_attn_Wo, L0_attn_bo)
    h = h + _L0_ffn_ref(_layernorm(h, axis=-1), L0_ffn_gate_w, L0_ffn_w_gate, L0_ffn_w_up, L0_ffn_w_down)
    return h

_drawn_inputs = setup_inputs


def setup_inputs(seed=0):
    import zlib

    import numpy as np

    out = dict(_drawn_inputs(seed))
    spreads = {'L0_attn_bq': (0.0, 2.0),
     'L0_attn_bk': (0.0, 2.0),
     'L0_attn_bv': (0.0, 0.1),
     'L0_attn_bo': (0.0, 0.1)}
    factors = {}
    for name, (base, spread) in spreads.items():
        noise = np.random.default_rng([zlib.crc32(name.encode()), seed]).standard_normal(out[name].shape)
        drawn = base * np.exp(spread * noise) if base else spread * noise
        out[name] = jnp.asarray(drawn.astype(out[name].dtype))
    for name, factor in factors.items():
        out[name] = (out[name] * factor).astype(out[name].dtype)
    return out
```

```python
from contextlib import ExitStack

import numpy as np

import concourse.bass as bass
from concourse import mybir

F32 = mybir.dt.float32
BF16 = mybir.dt.bfloat16
I32 = mybir.dt.int32
U32 = mybir.dt.uint32
ALU = mybir.AluOpType
ACT = mybir.ActivationFunctionType
AX_X = mybir.AxisListType.X

P = 128
IMAGES = 64
PAIRS = IMAGES // 2
PATCHES = 36
CLS_AT = PATCHES
TXT = 77
TOK = PATCHES + 1 + TXT
TOKENS = IMAGES * TOK
D = 256
KC = D // P
FEAT = 768
FC = FEAT // P
HEADS = 16
DH = D // HEADS
HPC = P // DH
KVW = P + HPC
EXPERTS = 8
INNER = 128
REGION = TOKENS + P
ROW = D + 4
MEAN, GAIN, ID = D, D + 1, D + 2
TILES = (TOKENS + EXPERTS * (P - 1)) // P
NO_TOKEN = 1 << 20
LN_EPS = 1e-5
Z_EPS = 1e-6

CONSTS = {
    "c_ident": (P, P), "c_earlier": (TOK, TOK), "c_mask": (P, KVW), "c_weight8": (TOK, 2 * EXPERTS),
    "c_region": (TOK, EXPERTS), "c_regcol": (EXPERTS, 1), "c_tri": (EXPERTS, 2 * EXPERTS),
    "c_slot": (1, TILES * EXPERTS), "c_slotrow": (1, TILES),
}


class Turn:

    def __init__(self, m, c):
        self.m, self.c, self.fixed = m, c, isinstance(m, int)
        self.n = 4 * m + c

    def __add__(self, k):
        return Turn(self.m, self.c + k)

    def __sub__(self, k):
        return Turn(self.m, self.c - k)

    def had(self, back):
        return not self.fixed or self.n - back >= 0

    def within(self, count):
        return not self.fixed or 0 <= self.n < count

    def upto(self, back=0, per=1):
        return per * (self.n - back + 1)

    def slot(self, ring):
        return self.c % ring

    def rounds(self, ring, back=0):
        return self.m * (4 // ring) + (self.c - back) // ring + 1


def build(nc, x, txt, w_tok, pos, tok_b, cls, wq, bq, wkv, bkv, wo, bo, gate, wgu, wdown, ids, consts, out):
    scratch = nc.dram_tensor("sorted_rows", (EXPERTS * REGION + P, ROW), F32, kind="Internal").ap()

    with ExitStack() as ctx:
        def sb(name, shape, dt=F32):
            return ctx.enter_context(nc.sbuf_tensor(name, shape, dt))

        def ps(name, shape):
            return ctx.enter_context(nc.psum_tensor(name, shape, F32))

        def sem(name):
            return ctx.enter_context(nc.semaphore(name))

        rows_all = sb("rows_all", [P, TILES, ROW])
        w_tok_s = sb("w_tok_s", [P, FC, D])
        wq_s = sb("wq_s", [P, KC, D])
        wkv_s = sb("wkv_s", [P, KC, 2 * D])
        wo_s = sb("wo_s", [P, KC, D])
        gate_s = sb("gate_s", [P, KC, EXPERTS])
        wgu_s = sb("wgu_s", [P, EXPERTS, KC, 2 * INNER])
        wdown_s = sb("wdown_s", [P, EXPERTS, D])
        bq_s = sb("bq_s", [P, KC])
        tokb_s = sb("tokb_s", [P, KC])
        cls_s = sb("cls_s", [P, KC])
        pos_s = sb("pos_s", [P, KC, PATCHES + 1])
        posb = sb("posb", [P, KC, PATCHES])
        bias_row = sb("bias_row", [1, 3 * D])
        bias_left = sb("bias_left", [1, 3 * D])
        bias_part = sb("bias_part", [1, 3, 3 * D], BF16)
        bias3 = sb("bias3", [P, 3 * D], BF16)
        ones_bf = sb("ones_bf", [P, TOK], BF16)
        ones = sb("ones", [P, TOK])
        half_neg = sb("half_neg", [P, 2])
        ids_s = sb("ids_s", [TOK, IMAGES], I32)
        tail_rows = sb("tail_rows", [P, ROW])
        con = {k: sb(k, list(s)) for k, s in CONSTS.items()}
        ident, mask, earlier = con["c_ident"], con["c_mask"], con["c_earlier"]

        x_in = sb("x_in", [P, 2, FC, 2 * PATCHES])
        tokT = sb("tokT", [P, KC, 2, PATCHES + 1])
        stats1 = sb("stats1", [TOK, 2, 6])
        mv1 = sb("mv1", [TOK, 2, 2, 2])
        ve1 = sb("ve1", [TOK, 2])
        rstd1 = sb("rstd1", [TOK, 2, 2])
        xn = sb("xn", [TOK, 2, 2, D])
        xnT = sb("xnT", [P, 2, KC, 2 * TOK])
        q_exp = sb("q_exp", [P, KC, 2 * TOK])
        q_relu = sb("q_relu", [P, KC, 2 * TOK])
        qT = sb("qT", [P, 2, KC, 2 * TOK])
        k_exp = sb("k_exp", [TOK, 2, D])
        k_relu = sb("k_relu", [TOK, 2, D])
        k_sb = sb("k_sb", [TOK, 2, 2, D])
        v_sb = sb("v_sb", [TOK, 2, 2, KC, KVW])
        kv_sb = sb("kv_sb", [P, 2, KC, KVW])
        den = sb("den", [TOK, 2, HEADS])
        z = sb("z", [TOK, 2, HEADS])
        attn = sb("attn", [TOK, 2, D])
        attnT = sb("attnT", [P, KC, 2 * TOK])
        rows = sb("rows", [TOK, 4, 2, ROW])
        stats2 = sb("stats2", [TOK, 2, 6])
        mv2 = sb("mv2", [TOK, 4, 2, 2])
        ve2 = sb("ve2", [TOK, 2])
        rstd2 = sb("rstd2", [TOK, 4, 2])
        xn2 = sb("xn2", [TOK, 2, D])
        xn2T = sb("xn2T", [P, KC, 2 * TOK])
        top = sb("top", [TOK, 2, 2])
        tied = sb("tied", [TOK, 2, EXPERTS])
        ranked = sb("ranked", [TOK, 2, EXPERTS])
        first = sb("first", [TOK, 2])
        chosen = sb("chosen", [TOK, 2, 2, EXPERTS])
        so_far = sb("so_far", [TOK, 2, EXPERTS])
        so_far_mid = sb("so_far_mid", [TOK, EXPERTS])
        exp_top = sb("exp_top", [TOK, 2, 2])
        one_plus = sb("one_plus", [TOK, 2])
        route_w = sb("route_w", [TOK, 2])
        place_e = sb("place_e", [TOK, 2, EXPERTS])
        place_f = sb("place_f", [TOK, 4, 2])
        place = sb("place", [TOK, 4, 2], I32)

        row_end = sb("row_end", [EXPERTS, 1])
        held = sb("held", [EXPERTS, 1])
        held_i = sb("held_i", [EXPERTS, 1], I32)
        tiles_i = sb("tiles_i", [EXPERTS, 1], I32)
        tiles_f = sb("tiles_f", [EXPERTS, 1])
        ends = sb("ends", [1, 2 * EXPERTS])
        tail_at = sb("tail_at", [1, EXPERTS], I32)
        past = sb("past", [1, TILES, EXPERTS])
        past_n = sb("past_n", [1, TILES, EXPERTS])
        slot_e = sb("slot_e", [1, TILES])
        slot_s = sb("slot_s", [1, TILES])
        slot_r = sb("slot_r", [1, TILES])
        slot_r2 = sb("slot_r2", [1, TILES])
        slot_row = sb("slot_row", [1, TILES], I32)
        slot_expert = sb("slot_expert", [1, TILES], I32)

        xs = sb("xs", [P, 2, D])
        xsT = sb("xsT", [P, 2, KC, P])
        silu_g = sb("silu_g", [P, 2, INNER])
        act_u = sb("act_u", [P, 2, INNER])
        actT = sb("actT", [P, 2, P])
        result = sb("result", [P, 4, D])
        result_id = sb("result_id", [P, 4], I32)

        b_tok = ps("b_tok", [P, 512])
        b_turn = ps("b_turn", [P, 512])
        b_qo = ps("b_qo", [P, 512])
        b_kvp = ps("b_kvp", [P, 2, 512])
        b_att = ps("b_att", [P, 2, 512])
        b_gate = ps("b_gate", [P, 512])

        b_x, b_gu = (b_tok[:, :], b_turn[:, :]), (b_kvp[:, 0, :], b_kvp[:, 1, :])
        b_a, b_y = (b_qo[:, :], b_gate[:, :]), (b_att[:, 0, :], b_att[:, 1, :])

        def b_tile(banks, t, width, start=0):
            return banks[t.slot(2)][:, start:start + width]

        s_const = sem("s_const")
        s_first = sem("s_first")
        s_weights = sem("s_weights")
        s_expert_w = sem("s_expert_w")
        s_bias_dma = sem("s_bias_dma")
        s_in = [sem(f"s_in{k}") for k in range(2)]
        s_prep = sem("s_prep")
        s_posb = sem("s_posb")
        s_bias = sem("s_bias")
        s_bias_chain = sem("s_bias_chain")
        tok_done = sem("tok_done")
        tokT_ready = sem("tokT_ready")
        back_done = sem("back_done")
        h_ready = sem("h_ready")
        stats1_done = sem("stats1_done")
        mv1_ready = sem("mv1_ready")
        ve1_done = sem("ve1_done")
        rstd1_ready = sem("rstd1_ready")
        xn_ready = sem("xn_ready")
        turn_done = sem("turn_done")
        xnT_ready = sem("xnT_ready")
        q_done = sem("q_done")
        q_parts = sem("q_parts")
        q_ready = sem("q_ready")
        kvp_done = sem("kvp_done")
        kv_parts = sem("kv_parts")
        k_ready = sem("k_ready")
        kvm_done = sem("kvm_done")
        kv_ready = sem("kv_ready")
        apply_done = sem("apply_done")
        den_done = sem("den_done")
        z_done = sem("z_done")
        attn_ready = sem("attn_ready")
        turn_attn_done = sem("turn_attn_done")
        attnT_ready = sem("attnT_ready")
        wo_done = sem("wo_done")
        h2_ready = sem("h2_ready")
        stats2_done = sem("stats2_done")
        mv2_ready = sem("mv2_ready")
        ve2_done = sem("ve2_done")
        rstd2_ready = sem("rstd2_ready")
        xn2_ready = sem("xn2_ready")
        turn2_done = sem("turn2_done")
        xn2T_ready = sem("xn2T_ready")
        gate_done = sem("gate_done")
        top_ready = sem("top_ready")
        route_step = sem("route_step")
        chosen_ready = sem("chosen_ready")
        exp_top_ready = sem("exp_top_ready")
        rank_done = sem("rank_done")
        place_step = sem("place_step")
        place_ready = sem("place_ready")
        fields_ready = sem("fields_ready")
        scattered = [sem(f"scattered{k}") for k in range(4)]
        table_pe = sem("table_pe")
        table_step = sem("table_step")
        table_ready = sem("table_ready")
        tail_zeroed = sem("tail_zeroed")
        row_loaded = [sem(f"row_loaded{k}") for k in range(4)]
        xs_ready = sem("xs_ready")
        turn_x_done = sem("turn_x_done")
        xsT_ready = sem("xsT_ready")
        gu_done = sem("gu_done")
        silu_ready = sem("silu_ready")
        act_ready = sem("act_ready")
        turn_a_done = sem("turn_a_done")
        actT_ready = sem("actT_ready")
        down_done = sem("down_done")
        result_ready = sem("result_ready")
        id_copied = sem("id_copied")
        stored = [sem(f"stored{k}") for k in range(4)]

        FIRST_DMAS, WEIGHT_DMAS, EXPERT_DMAS = 5, 4 + 2, 2
        STEADY_A, STEADY_B = (2, 7), (1, 15)
        BEFORE_A, AFTER_A = range(-3, 4 * STEADY_A[0]), range(4 * STEADY_A[1], PAIRS + 5)
        BEFORE_B, AFTER_B = range(-2, 4 * STEADY_B[0]), range(4 * STEADY_B[1], TILES + 2)

        def ahead(eng, value):
            return value if isinstance(value, int) else eng.to_reg(value)

        def walk(eng, before, steady, after, step):
            for i in before:
                step(Turn(0, i))
            with eng.Fori(steady[0], steady[1]) as m:
                for c in range(4):
                    step(Turn(m, c))
            for i in after:
                step(Turn(0, i))

        block = ctx.enter_context(nc.Block())

        @block.sync
        def _(sp):
            def load(p):
                if p.had(2):
                    sp.wait_ge(tok_done, p.upto(2))
                k = p.slot(2)
                sp.dma_start(x_in[:, k], x[bass.ds(p.n, 1)]).then_inc(s_in[k], 16)
                sp.dma_start(rows_all[CLS_AT + 1:TOK, bass.ds(2 * p.n, 2), 0:D],
                             txt[:, bass.ds(2 * p.n, 2)]).then_inc(s_in[k], 16)

            sp.dma_start(w_tok_s[:], w_tok).then_inc(s_first, 16)
            load(Turn(0, 0))
            sp.dma_start(pos_s[:], pos).then_inc(s_first, 16)
            sp.dma_start(tokb_s[:], tok_b).then_inc(s_first, 16)
            sp.dma_start(cls_s[:], cls).then_inc(s_first, 16)
            sp.dma_start(bq_s[:], bq).then_inc(s_first, 16)
            load(Turn(0, 1))
            sp.dma_start(wkv_s[:], wkv).then_inc(s_weights, 16)
            sp.dma_start(wq_s[:], wq).then_inc(s_weights, 16)
            sp.dma_start(wo_s[:], wo).then_inc(s_weights, 16)
            sp.dma_start(gate_s[:], gate).then_inc(s_weights, 16)
            for n in range(2, 4):
                load(Turn(0, n))
            with sp.Fori(1, PAIRS // 4) as m:
                for c in range(4):
                    load(Turn(m, c))

            sp.wait_ge(s_prep, 1)
            sp.dma_start(scratch[EXPERTS * REGION:EXPERTS * REGION + P, :], tail_rows[:]).then_inc(tail_zeroed, 16)
            sp.wait_ge(table_ready, 1)
            for e in range(EXPERTS):
                at = sp.value_load(tail_at[0:1, e:e + 1], min_val=0, max_val=EXPERTS * REGION - P)
                sp.dma_start(scratch[bass.ds(at, P), :], tail_rows[:]).then_inc(tail_zeroed, 16)
            sp.wait_ge(tail_zeroed, 16 * (EXPERTS + 1))
            for k in range(4):
                sp.wait_ge(scattered[k], 2 * 16 * PAIRS // 4)
            sp.wait_ge(h2_ready, PAIRS)
            sp.wait_ge(table_ready, 2)

            def load_tile(t, again):
                k = t.slot(4)
                if again:
                    sp.wait_ge(row_loaded[k], 16 * t.rounds(4, 4))
                at = sp.value_load(slot_row[0:1, bass.ds(t.n, 1)], min_val=0, max_val=EXPERTS * REGION)
                sp.dma_start(rows_all[:, bass.ds(t.n, 1), :], scratch[bass.ds(at, P), :]).then_inc(row_loaded[k], 16)

            for n in range(4):
                load_tile(Turn(0, n), False)
            with sp.Fori(1, TILES // 4) as m:
                for c in range(4):
                    load_tile(Turn(m, c), True)
            for k in range(4):
                sp.wait_ge(stored[k], 16 * TILES // 4)

        @block.gpsimd
        def _(pool):
            def rstd(mv, ve, to, ready, done, out_ready, p, ring):
                until = ahead(pool, p.upto())
                pool.wait_ge(s_prep, 1)
                pool.wait_ge(ready, until)
                nc.gpsimd.tensor_scalar(ve[:], mv[:, p.slot(ring), :, 1], LN_EPS, None, ALU.add).then_inc(done, 1)
                pool.wait_ge(done, p.upto())
                nc.gpsimd.tensor_tensor(to[:, p.slot(ring), :], ve[:], half_neg[0:TOK, :], ALU.pow).then_inc(out_ready, 1)

            def scatter(p):
                k = p.slot(4)
                until = ahead(pool, p.upto())
                pool.wait_ge(s_prep, 1)
                pool.wait_ge(place_ready, until)
                nc.gpsimd.tensor_copy(rows[:, k, :, MEAN], mv2[:, k, :, 0]).then_inc(fields_ready, 1)
                nc.gpsimd.tensor_copy(rows[:, k, :, ID].bitcast(I32), ids_s[:, bass.ds(2 * p.n, 2)]).then_inc(fields_ready, 1)
                nc.gpsimd.tensor_copy(place[:, k, :], place_f[:, k, :]).then_inc(fields_ready, 1)
                until = ahead(pool, p.upto(per=3))
                pool.wait_ge(s_prep, 1)
                pool.wait_ge(fields_ready, until)
                for b in range(2):
                    nc.gpsimd.indirect_dma_start(
                        out=scratch[0:EXPERTS * REGION, :],
                        out_offset=bass.IndirectOffsetOnAxis(ap=place[:, k, b:b + 1], axis=0),
                        in_=rows[:, k, b, :], in_offset=None).then_inc(scattered[k], 16)

            def step(i):
                if (i - 4).within(PAIRS):
                    scatter(i - 4)
                if (i - 2).within(PAIRS):
                    rstd(mv2, ve2, rstd2, mv2_ready, ve2_done, rstd2_ready, i - 2, 4)
                if (i + 3).within(PAIRS):
                    rstd(mv1, ve1, rstd1, mv1_ready, ve1_done, rstd1_ready, i + 3, 2)

            pool.wait_ge(s_const, 16 * (len(CONSTS) + 1))
            pool.wait_ge(s_prep, 1)
            walk(pool, BEFORE_A, STEADY_A, AFTER_A, step)

            def store(t):
                k = t.slot(4)
                until = ahead(pool, 16 * t.rounds(4, 4))
                until2 = ahead(pool, t.upto())
                pool.wait_ge(s_prep, 1)
                if t.had(4):
                    pool.wait_ge(stored[k], until)
                pool.wait_ge(result_ready, until2)
                nc.gpsimd.tensor_copy(result_id[:, k:k + 1], rows_all[:, bass.ds(t.n, 1), ID].bitcast(I32)).then_inc(id_copied, 1)
                until = ahead(pool, t.upto())
                pool.wait_ge(s_prep, 1)
                pool.wait_ge(id_copied, until)
                nc.gpsimd.indirect_dma_start(
                    out=out, out_offset=bass.IndirectOffsetOnAxis(ap=result_id[:, k:k + 1], axis=0),
                    in_=result[:, k, :], in_offset=None,
                    bounds_check=TOKENS - 1, oob_is_err=False).then_inc(stored[k], 16)

            walk(pool, BEFORE_B, STEADY_B, AFTER_B, lambda j: (j - 1).within(TILES) and store(j - 1))

        @block.scalar
        def _(act):
            for k, c in con.items():
                act.dma_start(c[:], consts[k]).then_inc(s_const, 16)
            act.dma_start(ids_s[:], ids).then_inc(s_const, 16)
            act.dma_start(bias_row[0:1, 0:2 * D], bkv).then_inc(s_weights, 16)
            act.dma_start(bias_row[0:1, 2 * D:3 * D], bo).then_inc(s_weights, 16)
            act.dma_start(wgu_s[:], wgu).then_inc(s_expert_w, 16)
            act.dma_start(wdown_s[:], wdown).then_inc(s_expert_w, 16)
            act.wait_ge(s_bias_chain, 6)
            for r in range(3):
                act.dma_start(bias3[r:r + 1, :], bias_part[:, r, :]).then_inc(s_bias_dma, 16)
            act.wait_ge(s_first, 16 * FIRST_DMAS)

            def step(i):
                if (i - 4).within(PAIRS):
                    p = i - 4
                    act.wait_ge(top_ready, p.upto())
                    if p.had(2):
                        act.wait_ge(place_ready, p.upto(2))
                    nc.scalar.activation(exp_top[:, p.slot(2), :], top[:, p.slot(2), :], ACT.Exp, scale=-1.0).then_inc(exp_top_ready, 1)
                if (i + 1).within(PAIRS):
                    p = i + 1
                    act.wait_ge(turn_done, p.upto())
                    if p.had(2):
                        act.wait_ge(q_done, p.upto(2))
                    nc.scalar.copy(xnT[:, p.slot(2)], b_turn[:, 0:4 * TOK].rearrange("p (k t) -> p k t", k=KC)).then_inc(xnT_ready, 1)
                if (i - 2).within(PAIRS):
                    p = i - 2
                    act.wait_ge(turn_attn_done, p.upto())
                    if p.had(1):
                        act.wait_ge(wo_done, p.upto(1))
                    nc.scalar.copy(attnT[:], b_gate[:, 0:4 * TOK].rearrange("p (k t) -> p k t", k=KC)).then_inc(attnT_ready, 1)
                if i.within(PAIRS):
                    p = i
                    act.wait_ge(kvp_done, p.upto())
                    if p.had(1):
                        act.wait_ge(k_ready, p.upto(1))
                    if p.had(2):
                        act.wait_ge(kvm_done, p.upto(2))
                    nc.scalar.activation(k_exp[:], b_kvp[0:TOK, :, 0:D], ACT.Exp)
                    nc.scalar.activation(k_relu[:], b_kvp[0:TOK, :, 0:D], ACT.Relu)
                    for b in range(2):
                        last = nc.scalar.copy(v_sb[:, p.slot(2), b, :, 0:P],
                                              b_kvp[0:TOK, b, D:2 * D].rearrange("p (k e) -> p k e", k=KC))
                    last.then_inc(kv_parts, 1)
                if (i - 3).within(PAIRS):
                    p = i - 3
                    act.wait_ge(turn2_done, p.upto())
                    if p.had(1):
                        act.wait_ge(gate_done, p.upto(1))
                    nc.scalar.copy(xn2T[:], b_turn[:, 0:4 * TOK].rearrange("p (k t) -> p k t", k=KC)).then_inc(xn2T_ready, 1)
                if i.within(PAIRS):
                    p = i
                    act.wait_ge(q_done, p.upto())
                    if p.had(1):
                        act.wait_ge(q_ready, p.upto(1))
                    for c in range(KC):
                        at = b_qo[:, c * 2 * TOK:(c + 1) * 2 * TOK]
                        nc.scalar.activation(q_exp[:, c, :], at, ACT.Exp, bias=bq_s[:, c:c + 1])
                        last = nc.scalar.activation(q_relu[:, c, :], at, ACT.Relu, bias=bq_s[:, c:c + 1])
                    last.then_inc(q_parts, 1)

            walk(act, BEFORE_A, STEADY_A, AFTER_A, step)

            def tile_step(j):
                if (j + 1).within(TILES):
                    t = j + 1
                    act.wait_ge(turn_x_done, t.upto())
                    if t.had(2):
                        act.wait_ge(gu_done, t.upto(2))
                    nc.scalar.copy(xsT[:, t.slot(2)], b_tile(b_x, t, KC * P).rearrange("p (k t) -> p k t", k=KC)).then_inc(xsT_ready, 1)
                if (j - 1).within(TILES):
                    t = j - 1
                    act.wait_ge(turn_a_done, t.upto())
                    if t.had(2):
                        act.wait_ge(down_done, t.upto(2))
                    nc.scalar.copy(actT[:, t.slot(2)], b_tile(b_a, t, P)).then_inc(actT_ready, 1)
                if j.within(TILES):
                    t = j
                    act.wait_ge(gu_done, t.upto())
                    if t.had(2):
                        act.wait_ge(act_ready, t.upto(2))
                    nc.scalar.activation(silu_g[:, t.slot(2)], b_tile(b_gu, t, INNER), ACT.Silu).then_inc(silu_ready, 1)

            walk(act, BEFORE_B, STEADY_B, AFTER_B, tile_step)

        @block.vector
        def _(dve):
            V = nc.vector
            V.memset(tail_rows[:, 0:ID], 0.0)
            V.memset(tail_rows[:, ID:].bitcast(I32), NO_TOKEN)
            V.memset(half_neg[:], -0.5)
            V.memset(ones[:], 1.0)
            V.memset(ones_bf[:], 1.0)
            V.memset(v_sb[:, :, :, :, P:].rearrange("p s b k w -> p (s b k) w"), 1.0)
            V.memset(bias3[:], 0.0)
            V.memset(rows[:, :, :, ID + 1:], 0.0).then_inc(s_prep, 1)
            dve.wait_ge(s_first, 16 * FIRST_DMAS)
            for c in range(KC):
                V.tensor_scalar(posb[:, c, :], pos_s[:, c, 1:], tokb_s[:, c:c + 1], None, ALU.add)
                for b in range(2):
                    last = V.tensor_tensor(tokT[:, c, b, PATCHES:], pos_s[:, c, 0:1], cls_s[:, c:c + 1], ALU.add)
            last.then_inc(s_posb, 1)
            dve.wait_ge(s_const, 16 * (len(CONSTS) + 1))
            V.tensor_copy(so_far[:, 0, :], con["c_region"][:]).then_inc(s_posb, 1)
            dve.wait_ge(s_weights, 16 * WEIGHT_DMAS)
            left = bias_row
            for r in range(3):
                V.tensor_copy(bias_part[:, r, :], left[:]).then_inc(s_bias_chain, 1)
                dve.wait_ge(s_bias_chain, 2 * r + 1)
                V.tensor_tensor(bias_left[:], left[:], bias_part[:, r, :], ALU.subtract).then_inc(s_bias_chain, 1)
                dve.wait_ge(s_bias_chain, 2 * r + 2)
                left = bias_left
            dve.wait_ge(s_posb, 2)

            def layernorm_stats(src, stats, mv, done, ready, p):
                for b in range(2):
                    last = V.bn_stats(stats[:, b, :], src(b))
                last.then_inc(done, 1)
                until = ahead(dve, p.upto())
                dve.wait_ge(s_posb, 2)
                dve.wait_ge(done, until)
                for b in range(2):
                    last = V.bn_aggr(mv[:, b, :], stats[:, b, :])
                last.then_inc(ready, 1)

            def step(i):
                if (i - 1).within(PAIRS):
                    p = i - 1
                    dve.wait_ge(kvm_done, p.upto())
                    if p.had(1):
                        dve.wait_ge(apply_done, p.upto(1))
                    V.tensor_tensor(kv_sb[:].rearrange("p b k w -> p (b k) w"),
                                    b_att[:, :, 0:KC * KVW].rearrange("p b (k w) -> p b k w", k=KC),
                                    mask[:].rearrange("p (a w) -> p a w", a=1).to_broadcast([P, 2 * KC, KVW]),
                                    ALU.mult).then_inc(kv_ready, 1)
                    dve.wait_ge(q_parts, p.upto())
                    if p.had(2):
                        dve.wait_ge(apply_done, p.upto(2))
                    V.scalar_tensor_tensor(qT[:, p.slot(2)], q_exp[:], 1.0, q_relu[:], ALU.min, ALU.add).then_inc(q_ready, 1)
                if (i + 2).within(PAIRS):
                    p = i + 2
                    dve.wait_ge(rstd1_ready, p.upto())
                    if p.had(2):
                        dve.wait_ge(turn_done, p.upto(2))
                    for b in range(2):
                        last = V.tensor_scalar(xn[:, p.slot(2), b, :], rows_all[0:TOK, bass.ds(2 * p.n + b, 1), 0:D],
                                               mv1[:, p.slot(2), b, 0:1], rstd1[:, p.slot(2), b:b + 1],
                                               ALU.subtract, ALU.mult)
                    last.then_inc(xn_ready, 1)
                if (i - 4).within(PAIRS):
                    p = i - 4
                    k = p.slot(4)
                    dve.wait_ge(exp_top_ready, p.upto())
                    V.tensor_scalar(one_plus[:], exp_top[:, p.slot(2), :], 1.0, None, ALU.add).then_inc(place_step, 1)
                    dve.wait_ge(rank_done, p.upto())
                    V.tensor_tensor(place_e[:], b_tok[0:TOK, 0:2 * EXPERTS].rearrange("p (b e) -> p b e", b=2),
                                    chosen[:, p.slot(2)], ALU.mult).then_inc(place_step, 1)
                    dve.wait_ge(place_step, p.upto(1, 4) + 1)
                    V.reciprocal(route_w[:], one_plus[:]).then_inc(place_step, 1)
                    dve.wait_ge(place_step, p.upto(1, 4) + 2)
                    V.tensor_reduce(place_f[:, k, :], place_e[:], AX_X, ALU.add).then_inc(place_step, 1)
                    dve.wait_ge(place_step, p.upto(0, 4))
                    V.tensor_tensor(rows[:, k, :, GAIN], route_w[:], rstd2[:, k, :], ALU.mult).then_inc(place_ready, 1)
                if (i - 2).within(PAIRS):
                    p = i - 2
                    k = p.slot(4)
                    dve.wait_ge(wo_done, p.upto())
                    if p.had(4):
                        dve.wait_ge(scattered[k], 32 * p.rounds(4, 4))
                    V.tensor_tensor(rows[:, k, :, 0:D], b_qo[0:TOK, 0:2 * D].rearrange("p (b d) -> p b d", b=2),
                                    rows_all[0:TOK, bass.ds(2 * p.n, 2), 0:D], ALU.add).then_inc(h2_ready, 1)
                    until = ahead(dve, p.upto())
                    dve.wait_ge(s_posb, 2)
                    dve.wait_ge(h2_ready, until)
                    layernorm_stats(lambda b: rows[:, k, b, 0:D], stats2, mv2[:, k], stats2_done, mv2_ready, p)
                if i.within(PAIRS):
                    p = i
                    dve.wait_ge(kv_parts, p.upto())
                    if p.had(2):
                        dve.wait_ge(kvm_done, p.upto(2))
                    V.scalar_tensor_tensor(k_sb[:, p.slot(2)], k_exp[:], 1.0, k_relu[:], ALU.min, ALU.add).then_inc(k_ready, 1)
                if (i - 1).within(PAIRS):
                    p = i - 1
                    dve.wait_ge(apply_done, p.upto())
                    heads = b_att[0:TOK, :, 0:KC * KVW].rearrange("p b (k w) -> p b k w", k=KC)
                    for b in range(2):
                        last = V.tensor_scalar(den[:, b, :].rearrange("p (k h) -> p k h", k=KC), heads[:, b, :, P:KVW],
                                               Z_EPS, None, ALU.add)
                    last.then_inc(den_done, 1)
                    dve.wait_ge(den_done, p.upto())
                    V.reciprocal(z[:], den[:]).then_inc(z_done, 1)
                    dve.wait_ge(z_done, p.upto())
                    if p.had(1):
                        dve.wait_ge(turn_attn_done, p.upto(1))
                    for b in range(2):
                        for c in range(KC):
                            last = V.tensor_tensor(
                                attn[:, b, c * P:(c + 1) * P].rearrange("p (h e) -> p h e", h=HPC),
                                heads[:, b, c, 0:P].rearrange("p (h e) -> p h e", h=HPC),
                                z[:, b, c * HPC:(c + 1) * HPC].rearrange("p (h a) -> p h a", a=1).to_broadcast([TOK, HPC, DH]),
                                ALU.mult)
                    last.then_inc(attn_ready, 1)
                if (i + 3).within(PAIRS):
                    p = i + 3
                    dve.wait_ge(tok_done, p.upto())
                    if p.had(1):
                        dve.wait_ge(back_done, p.upto(1))
                    for c in range(KC):
                        last = V.tensor_tensor(
                            tokT[:, c, :, 0:PATCHES],
                            b_tok[:, c * 2 * PATCHES:(c + 1) * 2 * PATCHES].rearrange("p (b n) -> p b n", b=2),
                            posb[:, c:c + 1, :].to_broadcast([P, 2, PATCHES]), ALU.add)
                    last.then_inc(tokT_ready, 1)
                if (i - 2).within(PAIRS):
                    p = i - 2
                    k = p.slot(4)
                    dve.wait_ge(rstd2_ready, p.upto())
                    if p.had(1):
                        dve.wait_ge(turn2_done, p.upto(1))
                    for b in range(2):
                        last = V.tensor_scalar(xn2[:, b, :], rows[:, k, b, 0:D], mv2[:, k, b, 0:1], rstd2[:, k, b:b + 1],
                                               ALU.subtract, ALU.mult)
                    last.then_inc(xn2_ready, 1)
                if (i + 3).within(PAIRS):
                    p = i + 3
                    dve.wait_ge(back_done, p.upto())
                    V.tensor_copy(rows_all[0:PATCHES + 1, bass.ds(2 * p.n, 2), 0:D],
                                  b_tok[0:PATCHES + 1, :].rearrange("p (b d) -> p b d", b=2)).then_inc(h_ready, 1)
                    until = ahead(dve, p.upto())
                    until2 = ahead(dve, 32 * p.rounds(2))
                    until3 = ahead(dve, p.upto(2))
                    dve.wait_ge(s_posb, 2)
                    dve.wait_ge(h_ready, until)
                    dve.wait_ge(s_in[p.slot(2)], until2)
                    if p.had(2):
                        dve.wait_ge(rstd1_ready, until3)
                    layernorm_stats(lambda b: rows_all[0:TOK, bass.ds(2 * p.n + b, 1), 0:D], stats1, mv1[:, p.slot(2)],
                                    stats1_done, mv1_ready, p)
                if (i - 3).within(PAIRS):
                    p = i - 3
                    dve.wait_ge(gate_done, p.upto())
                    if p.had(2):
                        dve.wait_ge(exp_top_ready, p.upto(2))
                    logits = b_gate[0:TOK, 0:2 * EXPERTS].rearrange("p (b e) -> p b e", b=2)

                    def over_experts(ap):
                        return ap.rearrange("p (b a) -> p b a", a=1).to_broadcast([TOK, 2, EXPERTS])

                    V.tensor_reduce(top[:, p.slot(2), :], logits, AX_X, ALU.max).then_inc(top_ready, 1)
                    dve.wait_ge(top_ready, p.upto())
                    V.tensor_tensor(tied[:], logits, over_experts(top[:, p.slot(2), :]), ALU.is_equal).then_inc(route_step, 1)
                    dve.wait_ge(route_step, p.upto(1, 4) + 1)
                    V.tensor_tensor(ranked[:], tied[:], con["c_weight8"][:].rearrange("p (b e) -> p b e", b=2),
                                    ALU.mult).then_inc(route_step, 1)
                    dve.wait_ge(route_step, p.upto(1, 4) + 2)
                    V.tensor_reduce(first[:], ranked[:], AX_X, ALU.max).then_inc(route_step, 1)
                    dve.wait_ge(route_step, p.upto(1, 4) + 3)
                    if p.had(1):
                        dve.wait_ge(rank_done, p.upto(1))
                    V.tensor_tensor(chosen[:, p.slot(2)], ranked[:], over_experts(first[:]), ALU.is_equal).then_inc(route_step, 1)
                    dve.wait_ge(route_step, p.upto(0, 4))
                    V.tensor_tensor(so_far_mid[:], so_far[:, p.slot(2), :], chosen[:, p.slot(2), 0, :], ALU.add).then_inc(chosen_ready, 1)
                    dve.wait_ge(chosen_ready, p.upto(1, 2) + 1)
                    V.tensor_tensor(so_far[:, (p + 1).slot(2), :], so_far_mid[:], chosen[:, p.slot(2), 1, :], ALU.add).then_inc(chosen_ready, 1)

            walk(dve, BEFORE_A, STEADY_A, AFTER_A, step)

            done = [0]

            def link(ins):
                ins.then_inc(table_step, 1)
                done[0] += 1
                dve.wait_ge(table_step, done[0])

            dve.wait_ge(table_pe, 1)
            link(V.tensor_copy(row_end[:], b_tok[0:EXPERTS, 0:1]))
            link(V.tensor_scalar(held[:], row_end[:], con["c_regcol"][:, 0:1], float(P - 1), ALU.subtract, ALU.add))
            link(V.tensor_copy(held_i[:], held[:]))
            link(V.tensor_scalar(tiles_i[:], held_i[:], P.bit_length() - 1, None, ALU.logical_shift_right))
            link(V.tensor_copy(tiles_f[:], tiles_i[:]))
            dve.wait_ge(table_pe, 2)
            link(V.tensor_copy(ends[:], b_turn[0:1, 0:2 * EXPERTS]))
            V.tensor_copy(tail_at[:], b_turn[0:1, 2 * EXPERTS:3 * EXPERTS]).then_inc(table_ready, 1)

            def over_slots(ap):
                return ap.rearrange("p (a e) -> p a e", a=1).to_broadcast([1, TILES, EXPERTS])

            link(V.tensor_tensor(past[:], con["c_slot"][:].rearrange("p (t e) -> p t e", t=TILES),
                                 over_slots(ends[:, 0:EXPERTS]), ALU.is_ge))
            link(V.tensor_reduce(slot_e[:], past[:], AX_X, ALU.add))
            link(V.tensor_tensor(past_n[:], past[:], over_slots(ends[:, EXPERTS:]), ALU.mult))
            link(V.tensor_reduce(slot_s[:], past_n[:], AX_X, ALU.add))
            link(V.scalar_tensor_tensor(slot_r[:], slot_s[:], -float(P), con["c_slotrow"][:], ALU.mult, ALU.add))
            link(V.scalar_tensor_tensor(slot_r2[:], slot_e[:], float(REGION), slot_r[:], ALU.mult, ALU.add))
            link(V.tensor_scalar(slot_row[:], slot_r2[:], float(EXPERTS * REGION), None, ALU.min))
            link(V.tensor_scalar(slot_expert[:], slot_e[:], float(EXPERTS - 1), None, ALU.min))
            V.memset(past[:], 0.0).then_inc(table_ready, 1)

            def tile_step(j):
                if (j + 2).within(TILES):
                    t = j + 2
                    dve.wait_ge(row_loaded[t.slot(4)], 16 * t.rounds(4))
                    if t.had(2):
                        dve.wait_ge(turn_x_done, t.upto(2))
                    at = rows_all[:, bass.ds(t.n, 1), :]
                    V.tensor_scalar(xs[:, t.slot(2)], at[:, :, 0:D], at[:, :, MEAN], at[:, :, GAIN],
                                    ALU.subtract, ALU.mult).then_inc(xs_ready, 1)
                if (j - 1).within(TILES):
                    t = j - 1
                    dve.wait_ge(down_done, t.upto())
                    if t.had(4):
                        dve.wait_ge(stored[t.slot(4)], 16 * t.rounds(4, 4))
                    V.tensor_tensor(result[:, t.slot(4)], b_tile(b_y, t, D), rows_all[:, bass.ds(t.n, 1), 0:D],
                                    ALU.add).then_inc(result_ready, 1)
                if j.within(TILES):
                    t = j
                    dve.wait_ge(silu_ready, t.upto())
                    if t.had(2):
                        dve.wait_ge(turn_a_done, t.upto(2))
                    V.tensor_tensor(act_u[:, t.slot(2)], b_tile(b_gu, t, INNER, INNER), silu_g[:, t.slot(2)],
                                    ALU.mult).then_inc(act_ready, 1)

            walk(dve, BEFORE_B, STEADY_B, AFTER_B, tile_step)

        @block.tensor
        def _(pe):
            T = nc.tensor

            def step(i):
                if (i - 1).within(PAIRS):
                    p = i - 1
                    pe.wait_ge(k_ready, p.upto())
                    if p.had(1):
                        pe.wait_ge(attn_ready, p.upto(1))
                    for b in range(2):
                        for c in range(KC):
                            last = T.matmul(b_att[:, b, c * KVW:(c + 1) * KVW], k_sb[:, p.slot(2), b, c * P:(c + 1) * P],
                                            v_sb[:, p.slot(2), b, c, :], start=True, stop=True)
                    last.then_inc(kvm_done, 1)
                if (i + 1).within(PAIRS):
                    p = i + 1
                    pe.wait_ge(xn_ready, p.upto())
                    if p.had(5):
                        pe.wait_ge(xn2T_ready, p.upto(5))
                    elif p.had(1):
                        pe.wait_ge(xnT_ready, p.upto(1))
                    for k in range(KC):
                        for b in range(2):
                            at = (2 * k + b) * TOK
                            last = T.transpose(b_turn[:, at:at + TOK], xn[:, p.slot(2), b, k * P:(k + 1) * P], ident[0:TOK, 0:TOK])
                    last.then_inc(turn_done, 1)
                if (i - 4).within(PAIRS):
                    p = i - 4
                    pe.wait_ge(chosen_ready, p.upto(per=2))
                    if (p + 6).within(PAIRS):
                        pe.wait_ge(h_ready, p.upto(-6))
                    else:
                        pe.wait_ge(place_ready, p.upto(1))
                    ranks = b_tok[0:TOK, 0:2 * EXPERTS]
                    T.matmul(ranks, earlier[:], chosen[:, p.slot(2)].rearrange("p b e -> p (b e)"), start=True, stop=False)
                    T.matmul(b_tok[0:TOK, EXPERTS:2 * EXPERTS], ones[0:TOK, :], chosen[:, p.slot(2), 0, :], start=False, stop=False)
                    T.matmul(b_tok[0:TOK, 0:EXPERTS], ones[0:TOK, :], so_far[:, p.slot(2), :], start=False, stop=False)
                    T.matmul(b_tok[0:TOK, EXPERTS:2 * EXPERTS], ones[0:TOK, :], so_far[:, p.slot(2), :],
                             start=False, stop=True).then_inc(rank_done, 1)
                if (i - 2).within(PAIRS):
                    p = i - 2
                    pe.wait_ge(attn_ready, p.upto())
                    if p.had(2):
                        pe.wait_ge(chosen_ready, p.upto(2, 2))
                    elif p.had(1):
                        pe.wait_ge(attnT_ready, p.upto(1))
                    for c in range(KC):
                        for b in range(2):
                            at = (2 * c + b) * TOK
                            last = T.transpose(b_gate[:, at:at + TOK], attn[:, b, c * P:(c + 1) * P], ident[0:TOK, 0:TOK])
                    last.then_inc(turn_attn_done, 1)
                if i.within(PAIRS):
                    p = i
                    pe.wait_ge(xnT_ready, p.upto())
                    if p.fixed and p.n == 0:
                        pe.wait_ge(s_bias_dma, 48)
                    if p.had(1):
                        pe.wait_ge(kv_parts, p.upto(1))
                    for b in range(2):
                        T.matmul(b_kvp[0:TOK, b, :], ones_bf[:, :], bias3[:, 0:2 * D], start=True, stop=False)
                        for k in range(KC):
                            last = T.matmul(b_kvp[0:TOK, b, :], xnT[:, p.slot(2), k, b * TOK:(b + 1) * TOK], wkv_s[:, k, :],
                                            start=False, stop=(k == KC - 1))
                    last.then_inc(kvp_done, 1)
                if (i - 2).within(PAIRS):
                    p = i - 2
                    pe.wait_ge(attnT_ready, p.upto())
                    if (p + 1).within(PAIRS):
                        pe.wait_ge(q_parts, p.upto(-1))
                    else:
                        pe.wait_ge(h2_ready, p.upto(1))
                    for b in range(2):
                        to = b_qo[0:TOK, b * D:(b + 1) * D]
                        T.matmul(to, ones_bf[:, :], bias3[:, 2 * D:3 * D], start=True, stop=False)
                        for c in range(KC):
                            last = T.matmul(to, attnT[:, c, b * TOK:(b + 1) * TOK], wo_s[:, c, :], start=False, stop=(c == KC - 1))
                    last.then_inc(wo_done, 1)
                if (i - 1).within(PAIRS):
                    p = i - 1
                    pe.wait_ge(kv_ready, p.upto())
                    pe.wait_ge(q_ready, p.upto())
                    for b in range(2):
                        for c in range(KC):
                            last = T.matmul(b_att[0:TOK, b, c * KVW:(c + 1) * KVW], qT[:, p.slot(2), c, b * TOK:(b + 1) * TOK],
                                            kv_sb[:, b, c, :], start=True, stop=True)
                    last.then_inc(apply_done, 1)
                if (i + 3).within(PAIRS):
                    p = i + 3
                    pe.wait_ge(s_in[p.slot(2)], 32 * p.rounds(2))
                    if p.had(7):
                        pe.wait_ge(place_ready, p.upto(7))
                    elif p.had(1):
                        pe.wait_ge(h_ready, p.upto(1))
                    for c in range(KC):
                        for k in range(FC):
                            last = T.matmul(b_tok[:, c * 2 * PATCHES:(c + 1) * 2 * PATCHES], w_tok_s[:, k, c * P:(c + 1) * P],
                                            x_in[:, p.slot(2), k, :], start=(k == 0), stop=(k == FC - 1))
                    last.then_inc(tok_done, 1)
                if (i - 3).within(PAIRS):
                    p = i - 3
                    pe.wait_ge(xn2_ready, p.upto())
                    if (p + 4).within(PAIRS):
                        pe.wait_ge(xnT_ready, p.upto(-4))
                    else:
                        pe.wait_ge(xn2T_ready, p.upto(1))
                    for k in range(KC):
                        for b in range(2):
                            at = (2 * k + b) * TOK
                            last = T.transpose(b_turn[:, at:at + TOK], xn2[:, b, k * P:(k + 1) * P], ident[0:TOK, 0:TOK])
                    last.then_inc(turn2_done, 1)
                if i.within(PAIRS):
                    p = i
                    if p.had(2):
                        pe.wait_ge(h2_ready, p.upto(2))
                    elif p.had(1):
                        pe.wait_ge(q_parts, p.upto(1))
                    for c in range(KC):
                        for k in range(KC):
                            last = T.matmul(b_qo[:, c * 2 * TOK:(c + 1) * 2 * TOK], wq_s[:, k, c * P:(c + 1) * P],
                                            xnT[:, p.slot(2), k, :], start=(k == 0), stop=(k == KC - 1))
                    last.then_inc(q_done, 1)
                if (i + 3).within(PAIRS):
                    p = i + 3
                    until = ahead(pe, p.upto())
                    pe.wait_ge(s_posb, 2)
                    pe.wait_ge(tokT_ready, until)
                    for b in range(2):
                        for c in range(KC):
                            at = b * D + c * P
                            last = T.transpose(b_tok[0:PATCHES + 1, at:at + P], tokT[:, c, b, :], ident[:])
                    last.then_inc(back_done, 1)
                if (i - 3).within(PAIRS):
                    p = i - 3
                    pe.wait_ge(xn2T_ready, p.upto())
                    if (p + 1).within(PAIRS):
                        pe.wait_ge(attnT_ready, p.upto(-1))
                    else:
                        pe.wait_ge(chosen_ready, p.upto(1, 2))
                    for b in range(2):
                        for k in range(KC):
                            last = T.matmul(b_gate[0:TOK, b * EXPERTS:(b + 1) * EXPERTS], xn2T[:, k, b * TOK:(b + 1) * TOK],
                                            gate_s[:, k, :], start=(k == 0), stop=(k == KC - 1))
                    last.then_inc(gate_done, 1)

            pe.wait_ge(s_first, 16 * FIRST_DMAS)
            pe.wait_ge(s_const, 16 * (len(CONSTS) + 1))
            pe.wait_ge(s_posb, 2)
            walk(pe, BEFORE_A, STEADY_A, AFTER_A, step)

            pe.wait_ge(place_ready, PAIRS)
            T.matmul(b_tok[0:EXPERTS, 0:2], so_far[:, PAIRS % 2, :], ones[0:TOK, 0:2], start=True, stop=True).then_inc(table_pe, 1)
            pe.wait_ge(table_step, 5)
            T.matmul(b_turn[0:1, 0:2 * EXPERTS], tiles_f[:], con["c_tri"][:], start=True, stop=True)
            T.matmul(b_turn[0:1, 2 * EXPERTS:3 * EXPERTS], row_end[:], ident[0:EXPERTS, 0:EXPERTS],
                     start=True, stop=True).then_inc(table_pe, 1)
            pe.wait_ge(table_ready, 2)
            pe.wait_ge(s_expert_w, 16 * EXPERT_DMAS)

            def tile_step(j):
                if (j + 1).within(TILES):
                    t = j + 1
                    pe.wait_ge(xs_ready, t.upto())
                    if t.had(2):
                        pe.wait_ge(xsT_ready, t.upto(2))
                    for k in range(KC):
                        last = T.transpose(b_tile(b_x, t, P, k * P), xs[:, t.slot(2), k * P:(k + 1) * P], ident[:])
                    last.then_inc(turn_x_done, 1)
                if (j - 1).within(TILES):
                    t = j - 1
                    pe.wait_ge(act_ready, t.upto())
                    if t.had(2):
                        pe.wait_ge(actT_ready, t.upto(2))
                    T.transpose(b_tile(b_a, t, P), act_u[:, t.slot(2)], ident[:]).then_inc(turn_a_done, 1)
                if j.within(TILES):
                    t = j
                    e = pe.value_load(slot_expert[0:1, bass.ds(t.n, 1)], min_val=0, max_val=EXPERTS - 1)
                    pe.wait_ge(xsT_ready, t.upto())
                    if t.had(2):
                        pe.wait_ge(act_ready, t.upto(2))
                    for k in range(KC):
                        last = T.matmul(b_tile(b_gu, t, 2 * INNER), xsT[:, t.slot(2), k, :], wgu_s[:, bass.ds(e, 1), k, :],
                                        start=(k == 0), stop=(k == KC - 1))
                    last.then_inc(gu_done, 1)
                if (j - 1).within(TILES):
                    t = j - 1
                    e = pe.value_load(slot_expert[0:1, bass.ds(t.n, 1)], min_val=0, max_val=EXPERTS - 1)
                    pe.wait_ge(actT_ready, t.upto())
                    if t.had(2):
                        pe.wait_ge(result_ready, t.upto(2))
                    T.matmul(b_tile(b_y, t, D), actT[:, t.slot(2)], wdown_s[:, bass.ds(e, 1), :], start=True, stop=True).then_inc(down_done, 1)

            walk(pe, BEFORE_B, STEADY_B, AFTER_B, tile_step)


def constants():
    f = np.float32
    d, h = np.arange(P), np.arange(HPC)
    own = (d[:, None] // DH == h[None, :]).astype(f)
    e = np.arange(EXPERTS)
    t = np.arange(TILES)
    return {
        "c_ident": np.eye(P, dtype=f),
        "c_earlier": np.triu(np.ones((TOK, TOK), f), 1),
        "c_mask": np.concatenate([np.repeat(own, DH, axis=1), own], axis=1),
        "c_weight8": np.tile((EXPERTS - e).astype(f), (TOK, 2)),
        "c_region": np.concatenate([(e * REGION).astype(f)[None], np.zeros((TOK - 1, EXPERTS), f)]),
        "c_regcol": (e * REGION).astype(f)[:, None],
        "c_tri": np.concatenate([np.triu(np.ones((EXPERTS, EXPERTS), f)), np.eye(EXPERTS, dtype=f)], axis=1),
        "c_slot": np.repeat(t, EXPERTS).astype(f)[None],
        "c_slotrow": (t * P).astype(f)[None],
    }


def token_ids():
    at = np.concatenate([np.arange(1, PATCHES + 1), [0], np.arange(PATCHES + 1, TOK)])
    return (np.arange(IMAGES)[None, :] * TOK + at[:, None]).astype(np.int32)


def kernel(**inputs):
    import numpy as _np
    import concourse.bacc as _bacc
    from concourse import mybir as _mybir
    from concourse.bass_utils import run_bass_kernel_spmd as _run

    v = {k.replace("L0_", ""): _np.asarray(a) for k, a in inputs.items()}

    def chunks(a):
        return a.reshape(-1, P, a.shape[-1]).transpose(1, 0, 2)

    px = 16
    patches = v["x"].reshape(PAIRS, 2, 3, 6, px, 6, px).transpose(0, 2, 4, 6, 1, 3, 5)
    layout = {
        "x": patches.reshape(PAIRS, FC, P, 2 * PATCHES).transpose(0, 2, 1, 3),
        "txt": v["txt"].transpose(1, 0, 2),
        "w_tok": chunks(v["tok_W"].T),
        "pos": chunks(v["tok_pos_enc"][0].T),
        "tok_b": v["tok_b"].reshape(KC, P).T,
        "cls": v["tok_cls_token"].reshape(KC, P).T,
        "wq": chunks(v["attn_Wq"].T),
        "bq": v["attn_bq"].reshape(KC, P).T,
        "wkv": chunks(_np.concatenate([v["attn_Wk"].T, v["attn_Wv"].T], axis=1)),
        "bkv": _np.concatenate([v["attn_bk"], v["attn_bv"]])[None],
        "wo": chunks(v["attn_Wo"].T),
        "bo": v["attn_bo"][None],
        "gate": chunks(v["ffn_gate_w"].T),
        "wgu": _np.concatenate([v["ffn_w_gate"], v["ffn_w_up"]], axis=1).transpose(2, 0, 1)
               .reshape(KC, P, EXPERTS, 2 * INNER).transpose(1, 2, 0, 3),
        "wdown": v["ffn_w_down"].transpose(2, 0, 1),
        "ids": token_ids(),
    }
    layout.update(constants())
    nc = _bacc.Bacc("TRN2", target_bir_lowering=False, num_devices=1)
    arrays, args = {}, {}
    for name, a in layout.items():
        a = _np.ascontiguousarray(a)
        arrays[f"in_{name}"] = a
        args[name] = nc.dram_tensor(f"in_{name}", a.shape, _mybir.dt.from_np(a.dtype), kind="ExternalInput").ap()
    out = nc.dram_tensor("out_0", (TOKENS, D), _mybir.dt.float32, kind="ExternalOutput").ap()
    consts = {k: args.pop(k) for k in CONSTS}
    build(nc, consts=consts, out=out, **args)
    r = _run(nc, [arrays], core_ids=[0])
    return r.results[0]["out_0"].reshape(IMAGES, TOK, D)
```

```python
from contextlib import ExitStack

import numpy as np

import concourse.bass as bass
from concourse import mybir

F32 = mybir.dt.float32
F32R = mybir.dt.float32r
BF16 = mybir.dt.bfloat16
I32 = mybir.dt.int32
U32 = mybir.dt.uint32
ALU = mybir.AluOpType
ACT = mybir.ActivationFunctionType
AX_X = mybir.AxisListType.X

P = 128
IMAGES = 64
PAIRS = IMAGES // 2
PATCHES = 36
CLS_AT = PATCHES
TXT = 77
TOK = PATCHES + 1 + TXT
TOKENS = IMAGES * TOK
D = 256
KC = D // P
FEAT = 768
FC = FEAT // P
HEADS = 16
DH = D // HEADS
HPC = P // DH
KVW = P + HPC
EXPERTS = 8
INNER = 128
REGION = TOKENS + P
ROW = D + 4
SHIFT, GAIN, ID = D, D + 1, D + 2
OCT = 8
QW = 256
TILES = (TOKENS + EXPERTS * (P - 1)) // P
NO_TOKEN = 1 << 20
LN_EPS = 1e-5
Z_EPS = 1e-6

CONSTS = {
    "c_ident": (P, P), "c_earlier": (TOK, TOK), "c_mask": (P, KVW), "c_weight8": (TOK, EXPERTS),
    "c_region": (P, 2 * EXPERTS), "c_regcol": (EXPERTS, 1), "c_tri": (EXPERTS, 2 * EXPERTS),
    "c_slot": (1, TILES * EXPERTS), "c_slotrow": (1, TILES),
}


class Turn:

    def __init__(self, m, c):
        self.m, self.c, self.fixed = m, c, isinstance(m, int)
        self.n = 4 * m + c

    def __add__(self, k):
        return Turn(self.m, self.c + k)

    def __sub__(self, k):
        return Turn(self.m, self.c - k)

    def had(self, back):
        return not self.fixed or self.n - back >= 0

    def within(self, count):
        return not self.fixed or 0 <= self.n < count

    def upto(self, back=0, per=1):
        return per * (self.n - back + 1)

    def slot(self, ring):
        return self.c % ring

    def rounds(self, ring, back=0):
        return self.m * (4 // ring) + (self.c - back) // ring + 1


def build(nc, x, txt, w_tok, pos, tok_b, cls, wq, bq, wkv, bkv, wo, bo, gate, wgu, wdown, ids, consts, out):
    scratch = nc.dram_tensor("sorted_rows", (EXPERTS * REGION + P, ROW), F32, kind="Internal").ap()

    with ExitStack() as ctx:
        def sb(name, shape, dt=F32, at=ctx):
            return at.enter_context(nc.sbuf_tensor(name, shape, dt))

        def parts(name, shape, at=ctx):
            return sb(name + "_hi", shape, F32R, at), sb(name + "_lo", shape, F32R, at)

        def ps(name, shape):
            return ctx.enter_context(nc.psum_tensor(name, shape, F32))

        def sem(name):
            return ctx.enter_context(nc.semaphore(name))

        rows_all = sb("rows_all", [P, TILES, ROW])
        wq_hi, wq_lo = parts("wq", [P, KC, D])
        wkv_hi, wkv_lo = parts("wkv", [P, KC, 2 * D])
        wo_hi, wo_lo = parts("wo", [P, KC, D])
        wgu_hi, wgu_lo = parts("wgu", [P, EXPERTS, KC, 2 * INNER])
        gate_s = sb("gate_s", [P, KC, EXPERTS])
        bq_s = sb("bq_s", [P, KC])
        tokb_s = sb("tokb_s", [P, KC])
        cls_s = sb("cls_s", [P, KC])
        pos_s = sb("pos_s", [P, KC, PATCHES + 1])
        posb = sb("posb", [P, KC, PATCHES])
        bias3 = sb("bias3", [P, 3 * D], BF16)
        ones_bf = sb("ones_bf", [P, TOK], BF16)
        earlier = sb("earlier", [TOK, TOK], BF16)
        half_neg = sb("half_neg", [P, 2])
        ids_s = sb("ids_s", [TOK, IMAGES], I32)
        tail_rows = sb("tail_rows", [P, ROW])
        con = {k: sb(k, list(s)) for k, s in CONSTS.items()}
        ident, mask = con["c_ident"], con["c_mask"]
        so_far = sb("so_far", [P, 2, 2, EXPERTS], BF16)

        with ExitStack() as early:
            tokT_all = sb("tokT_all", [P, KC, IMAGES, PATCHES], at=early)
        wdown_hi, wdown_lo = parts("wdown", [P, EXPERTS, D])
        sb("wdown_rest", [P, KC * IMAGES * PATCHES - 2 * EXPERTS * D])

        with ExitStack() as room:
            xp_hi, xp_lo = parts("xp", [P, 2, FC // 2, OCT * PATCHES], room)
            w_tok_hi, w_tok_lo = parts("w_tok", [P, FC, D], room)
            bias_row = sb("bias_row", [1, 3 * D], at=room)
            bias_left = sb("bias_left", [1, 3 * D], at=room)
            bias_part = sb("bias_part", [1, 3, 3 * D], BF16, room)

        with ExitStack() as room:
            tokT = sb("tokT", [P, KC, 2, PATCHES + 1], at=room)
            stats1 = sb("stats1", [TOK, 2, 6], at=room)
            mv1 = sb("mv1", [TOK, 2, 2, 2], at=room)
            ve1 = sb("ve1", [TOK, 2, 2], at=room)
            rstd1 = sb("rstd1", [TOK, 2, 2], at=room)
            shift1 = sb("shift1", [TOK, 2, 2], at=room)
            xn = sb("xn", [TOK, 2, D], at=room)
            xnT_hi, xnT_lo = parts("xnT", [P, 2, KC, QW], room)
            q_exp = sb("q_exp", [P, KC, 2 * TOK], at=room)
            q_relu = sb("q_relu", [P, KC, 2 * TOK], at=room)
            qT = sb("qT", [P, KC, 2 * TOK], at=room)
            k_exp = sb("k_exp", [TOK, 2, D], at=room)
            k_relu = sb("k_relu", [TOK, 2, D], at=room)
            k_sb = sb("k_sb", [TOK, 2, D], at=room)
            v_sb = sb("v_sb", [TOK, 2, KC, KVW], at=room)
            kv_sb = sb("kv_sb", [P, 2, KC, KVW], at=room)
            den = sb("den", [TOK, 2, HEADS], at=room)
            z = sb("z", [TOK, 2, HEADS], at=room)
            attn = sb("attn", [TOK, 2, D], at=room)
            attnT_hi, attnT_lo = parts("attnT", [P, KC, 2 * TOK], room)
            rows = sb("rows", [TOK, 4, 2, ROW], at=room)
            stats2 = sb("stats2", [TOK, 2, 6], at=room)
            mv2 = sb("mv2", [TOK, 4, 2, 2], at=room)
            ve2 = sb("ve2", [TOK, 2, 2], at=room)
            rstd2 = sb("rstd2", [TOK, 4, 2], at=room)
            shift2 = sb("shift2", [TOK, 4, 2], at=room)
            xn2 = sb("xn2", [TOK, 2, D], at=room)
            xn2T = sb("xn2T", [P, KC, 2 * TOK], at=room)
            top = sb("top", [TOK, 2, 2], at=room)
            ranked = sb("ranked", [TOK, 2, EXPERTS], at=room)
            first = sb("first", [TOK, 2], at=room)
            chosen = sb("chosen", [TOK, 2, 2, EXPERTS], BF16, room)
            tanh_top = sb("tanh_top", [TOK, 2, 2], at=room)
            route_w = sb("route_w", [TOK, 2], at=room)
            place_e = sb("place_e", [TOK, 2, EXPERTS], at=room)
            place_f = sb("place_f", [TOK, 4, 2], at=room)
            place = sb("place", [TOK, 4, 2], I32, room)

        with ExitStack() as room:
            row_end = sb("row_end", [EXPERTS, 1], at=room)
            held = sb("held", [EXPERTS, 1], at=room)
            held_i = sb("held_i", [EXPERTS, 1], I32, room)
            tiles_i = sb("tiles_i", [EXPERTS, 1], I32, room)
            tiles_f = sb("tiles_f", [EXPERTS, 1], at=room)
            ends = sb("ends", [1, 2 * EXPERTS], at=room)
            tail_at = sb("tail_at", [1, EXPERTS], I32, room)
            past = sb("past", [1, TILES, EXPERTS], at=room)
            past_n = sb("past_n", [1, TILES, EXPERTS], at=room)
            slot_e = sb("slot_e", [1, TILES], at=room)
            slot_s = sb("slot_s", [1, TILES], at=room)
            slot_r = sb("slot_r", [1, TILES], at=room)
            slot_r2 = sb("slot_r2", [1, TILES], at=room)
            slot_row = sb("slot_row", [1, TILES], I32, room)
            slot_expert = sb("slot_expert", [1, TILES], I32, room)
            xs = sb("xs", [P, 2, D], at=room)
            xsT_hi, xsT_lo = parts("xsT", [P, 4, KC, P], room)
            silu_g = sb("silu_g", [P, 2, INNER], at=room)
            act_u = sb("act_u", [P, 2, INNER], at=room)
            actT_hi, actT_lo = parts("actT", [P, 2, P], room)
            result = sb("result", [P, 4, D], at=room)
            result_id = sb("result_id", [P, 4], I32, room)
            affine = sb("affine", [P, 4, 2], at=room)

        staging = rows_all[:, TILES // 2:, :].rearrange("p t w -> p (t w)")
        X_UNIT = (FC // 2) * OCT * PATCHES
        sizes = [4 * X_UNIT, FC * D, KC * 2 * D, KC * D, KC * D]
        starts = [sum(sizes[:n]) for n in range(len(sizes) + 1)]
        assert starts[-1] <= staging.shape[1]
        x_in, w_tok_raw, wkv_raw, wq_raw, wo_raw = (staging[:, a:b] for a, b in zip(starts, starts[1:]))
        GU, DOWN = KC * 2 * INNER, D
        expert_raw = rows_all[:, 0:TILES // 2, :].rearrange("p t w -> p (t w)")[:, 0:EXPERTS * (GU + DOWN)]
        RAW_PAIRS = -(-EXPERTS * (GU + DOWN) // (2 * ROW))

        b_tok = ps("b_tok", [P, 512])
        b_turn = ps("b_turn", [P, 512])
        b_qo = ps("b_qo", [P, 512])
        b_kvp = ps("b_kvp", [P, 2, 512])
        b_att = ps("b_att", [P, 2, 512])
        b_gate = ps("b_gate", [P, 512])
        b_x, b_gu = (b_tok[:, :], b_turn[:, :]), (b_kvp[:, 0, :], b_kvp[:, 1, :])
        b_a, b_y = (b_qo[:, :], b_gate[:, :]), (b_att[:, 0, :], b_att[:, 1, :])

        def b_tile(banks, t, width, start=0):
            return banks[t.slot(2)][:, start:start + width]

        s_const = sem("s_const")
        s_tokw = sem("s_tokw")
        s_small = sem("s_small")
        s_weights = sem("s_weights")
        s_expert_w = sem("s_expert_w")
        s_bias_dma = sem("s_bias_dma")
        s_prep = sem("s_prep")
        s_posb = sem("s_posb")
        s_bias_chain = sem("s_bias_chain")
        w_hi = sem("w_hi")
        w_lo = sem("w_lo")
        x_loaded = [sem(f"x_loaded{k}") for k in range(4)]
        x_hi_ready = sem("x_hi_ready")
        x_lo_ready = sem("x_lo_ready")
        unit_done = sem("unit_done")
        patches_ready = sem("patches_ready")
        s_in = [sem(f"s_in{k}") for k in range(2)]
        tokT_ready = sem("tokT_ready")
        back_done = sem("back_done")
        h_ready = sem("h_ready")
        stats1_done = sem("stats1_done")
        mv1_ready = sem("mv1_ready")
        rstd1_step = sem("rstd1_step")
        xn_ready = sem("xn_ready")
        turn_done = sem("turn_done")
        xnT_hi_ready = sem("xnT_hi_ready")
        xnT_lo_ready = sem("xnT_lo_ready")
        q_done = sem("q_done")
        q_parts = sem("q_parts")
        q_ready = sem("q_ready")
        kvp_done = sem("kvp_done")
        kv_parts = sem("kv_parts")
        k_step = sem("k_step")
        k_ready = sem("k_ready")
        v_ready = sem("v_ready")
        room_ready = sem("room_ready")
        affine_ready = sem("affine_ready")
        kvm_done = sem("kvm_done")
        kv_ready = sem("kv_ready")
        apply_done = sem("apply_done")
        den_done = sem("den_done")
        z_done = sem("z_done")
        attn_ready = sem("attn_ready")
        turn_attn_done = sem("turn_attn_done")
        attnT_hi_ready = sem("attnT_hi_ready")
        attnT_lo_ready = sem("attnT_lo_ready")
        wo_done = sem("wo_done")
        h2_ready = sem("h2_ready")
        stats2_done = sem("stats2_done")
        mv2_ready = sem("mv2_ready")
        rstd2_step = sem("rstd2_step")
        xn2_ready = sem("xn2_ready")
        turn2_done = sem("turn2_done")
        xn2T_ready = sem("xn2T_ready")
        gate_done = sem("gate_done")
        top_ready = sem("top_ready")
        ranked_ready = sem("ranked_ready")
        first_ready = sem("first_ready")
        chosen_ready = sem("chosen_ready")
        so_far_ready = sem("so_far_ready")
        tanh_ready = sem("tanh_ready")
        rank_done = sem("rank_done")
        place_ready = sem("place_ready")
        field_step = sem("field_step")
        scattered = [sem(f"scattered{k}") for k in range(4)]
        expert_hi = sem("expert_hi")
        expert_lo = sem("expert_lo")
        table_pe = sem("table_pe")
        table_step = sem("table_step")
        table_ready = sem("table_ready")
        tail_zeroed = sem("tail_zeroed")
        row_loaded = [sem(f"row_loaded{k}") for k in range(4)]
        xs_ready = sem("xs_ready")
        turn_x_done = sem("turn_x_done")
        xsT_hi_ready = sem("xsT_hi_ready")
        xsT_lo_ready = sem("xsT_lo_ready")
        gu_done = sem("gu_done")
        silu_ready = sem("silu_ready")
        act_ready = sem("act_ready")
        turn_a_done = sem("turn_a_done")
        actT_hi_ready = sem("actT_hi_ready")
        actT_lo_ready = sem("actT_lo_ready")
        down_done = sem("down_done")
        result_ready = sem("result_ready")
        id_copied = sem("id_copied")
        stored = [sem(f"stored{k}") for k in range(4)]

        SMALL_DMAS, WEIGHT_DMAS = 5, 5
        CONST_DMAS = len(CONSTS) + 1
        UNITS = 2 * IMAGES // OCT
        STEADY_A, STEADY_B = (2, 7), (1, 15)
        BEFORE_A, AFTER_A = range(-3, 4 * STEADY_A[0]), range(4 * STEADY_A[1], PAIRS + 5)
        BEFORE_B, AFTER_B = range(-3, 4 * STEADY_B[0]), range(4 * STEADY_B[1], TILES + 3)
        FIRST_SPLIT = PAIRS - 3

        def ahead(eng, value):
            return value if isinstance(value, int) else eng.to_reg(value)

        def walk(eng, before, steady, after, step):
            for i in before:
                step(Turn(0, i))
            with eng.Fori(steady[0], steady[1]) as m:
                for c in range(4):
                    step(Turn(m, c))
            for i in after:
                step(Turn(0, i))

        def walk_units(eng, unit):
            walk(eng, range(4), (1, UNITS // 4), (), unit)

        block = ctx.enter_context(nc.Block())

        @block.sync
        def _(sp):
            def load_unit(u):
                k = u.slot(4)
                if u.had(4):
                    sp.wait_ge(x_lo_ready, u.upto(4))
                sp.dma_start(x_in[:, k * X_UNIT:(k + 1) * X_UNIT], x[bass.ds(u.n, 1)]).then_inc(x_loaded[k], 16)

            def load_text(p):
                if p.had(2):
                    sp.wait_ge(mv1_ready, p.upto(2))
                sp.dma_start(rows_all[CLS_AT + 1:TOK, bass.ds(2 * p.n, 2), 0:D],
                             txt[:, bass.ds(2 * p.n, 2)]).then_inc(s_in[p.slot(2)], 16)

            sp.dma_start(w_tok_raw[:, 0:3 * D], w_tok[:, 0:3 * D]).then_inc(s_tokw, 16)
            load_unit(Turn(0, 0))
            sp.dma_start(w_tok_raw[:, 3 * D:], w_tok[:, 3 * D:]).then_inc(s_tokw, 16)
            load_unit(Turn(0, 1))
            for n in (2, 3):
                load_unit(Turn(0, n))
            for n in (0, 1):
                load_text(Turn(0, n))
            with sp.Fori(1, UNITS // 4) as m:
                for c in range(4):
                    load_unit(Turn(m, c))
            for n in (2, 3):
                load_text(Turn(0, n))
            with sp.Fori(1, PAIRS // 4) as m:
                for c in range(4):
                    load_text(Turn(m, c))
            sp.wait_ge(h2_ready, RAW_PAIRS)
            for e in range(EXPERTS):
                at = e * (GU + DOWN)
                sp.dma_start(expert_raw[:, at:at + GU], wgu[:, e * GU:(e + 1) * GU]).then_inc(s_expert_w, 16)
                sp.dma_start(expert_raw[:, at + GU:at + GU + DOWN], wdown[:, e * DOWN:(e + 1) * DOWN]).then_inc(s_expert_w, 16)

            sp.wait_ge(s_prep, 1)
            sp.dma_start(scratch[EXPERTS * REGION:EXPERTS * REGION + P, :], tail_rows[:]).then_inc(tail_zeroed, 16)
            sp.wait_ge(table_ready, 1)
            for e in range(EXPERTS):
                at = sp.value_load(tail_at[0:1, e:e + 1], min_val=0, max_val=EXPERTS * REGION - P)
                sp.dma_start(scratch[bass.ds(at, P), :], tail_rows[:]).then_inc(tail_zeroed, 16)
            sp.wait_ge(tail_zeroed, 16 * (EXPERTS + 1))
            for k in range(4):
                sp.wait_ge(scattered[k], 2 * 16 * PAIRS // 4)
            sp.wait_ge(h2_ready, PAIRS)
            sp.wait_ge(expert_lo, EXPERTS)
            sp.wait_ge(table_ready, 2)

            def load_tile(t, again):
                k = t.slot(4)
                if again:
                    sp.wait_ge(row_loaded[k], 16 * t.rounds(4, 4))
                at = sp.value_load(slot_row[0:1, bass.ds(t.n, 1)], min_val=0, max_val=EXPERTS * REGION)
                sp.dma_start(rows_all[:, bass.ds(t.n, 1), :], scratch[bass.ds(at, P), :]).then_inc(row_loaded[k], 16)

            for n in range(4):
                load_tile(Turn(0, n), False)
            with sp.Fori(1, TILES // 4) as m:
                for c in range(4):
                    load_tile(Turn(m, c), True)
            for k in range(4):
                sp.wait_ge(stored[k], 16 * TILES // 4)

        @block.gpsimd
        def _(pool):
            G = nc.gpsimd

            def rstd(mv, ve, to, shift, ready, chain, p, ring):
                k = p.slot(ring)
                until = ahead(pool, p.upto())
                pool.wait_ge(s_prep, 1)
                pool.wait_ge(ready, until)
                G.tensor_scalar(ve[:, 0, :], mv[:, k, :, 1], LN_EPS, None, ALU.add).then_inc(chain, 1)
                G.tensor_scalar(ve[:, 1, :], mv[:, k, :, 0], -1.0, None, ALU.mult).then_inc(chain, 1)
                pool.wait_ge(chain, p.upto(1, 4) + 2)
                G.tensor_tensor(to[:, k, :], ve[:, 0, :], half_neg[0:TOK, :], ALU.pow).then_inc(chain, 1)
                pool.wait_ge(chain, p.upto(1, 4) + 3)
                G.tensor_tensor(shift[:, k, :], ve[:, 1, :], to[:, k, :], ALU.mult).then_inc(chain, 1)

            def scatter(p):
                k = p.slot(4)
                until = ahead(pool, p.upto())
                pool.wait_ge(s_prep, 1)
                pool.wait_ge(tanh_ready, until)
                G.tensor_scalar(route_w[:], tanh_top[:, p.slot(2), :], 1.0, 0.5, ALU.add, ALU.mult).then_inc(field_step, 1)
                G.tensor_copy(rows[:, k, :, ID].bitcast(I32), ids_s[:, bass.ds(2 * p.n, 2)]).then_inc(field_step, 1)
                pool.wait_ge(field_step, p.upto(1, 5) + 1)
                G.tensor_tensor(rows[:, k, :, GAIN], route_w[:], rstd2[:, k, :], ALU.mult).then_inc(field_step, 1)
                G.tensor_tensor(rows[:, k, :, SHIFT], route_w[:], shift2[:, k, :], ALU.mult).then_inc(field_step, 1)
                until = ahead(pool, p.upto())
                pool.wait_ge(s_prep, 1)
                pool.wait_ge(place_ready, until)
                G.tensor_copy(place[:, k, :], place_f[:, k, :]).then_inc(field_step, 1)
                until = ahead(pool, p.upto(0, 5))
                pool.wait_ge(s_prep, 1)
                pool.wait_ge(field_step, until)
                for b in range(2):
                    G.indirect_dma_start(
                        out=scratch[0:EXPERTS * REGION, :],
                        out_offset=bass.IndirectOffsetOnAxis(ap=place[:, k, b:b + 1], axis=0),
                        in_=rows[:, k, b, :], in_offset=None).then_inc(scattered[k], 16)

            def step(i):
                if (i - 4).within(PAIRS):
                    p = i - 4
                    pool.wait_ge(chosen_ready, p.upto())
                    if p.had(1):
                        pool.wait_ge(rank_done, p.upto(1))
                    G.tensor_tensor(so_far[0:TOK, (p + 1).slot(2)], so_far[0:TOK, p.slot(2)], chosen[:, p.slot(2)],
                                    ALU.add).then_inc(so_far_ready, 1)
                if (i + 3).within(PAIRS):
                    p = i + 3
                    until = ahead(pool, p.upto(1))
                    pool.wait_ge(s_prep, 1)
                    if p.had(1):
                        pool.wait_ge(back_done, until)
                    G.tensor_copy(tokT[:, :, :, 0:PATCHES], tokT_all[:, :, bass.ds(2 * p.n, 2), :]).then_inc(tokT_ready, 1)
                if (i + 2).within(PAIRS):
                    rstd(mv1, ve1, rstd1, shift1, mv1_ready, rstd1_step, i + 2, 2)
                if i.within(PAIRS):
                    p = i
                    until, until2 = ahead(pool, p.upto()), ahead(pool, p.upto(1))
                    pool.wait_ge(s_prep, 1)
                    pool.wait_ge(kv_parts, until)
                    if p.had(1):
                        pool.wait_ge(kvm_done, until2)
                    G.tensor_scalar(k_sb[:], k_exp[:], 1.0, None, ALU.min).then_inc(k_step, 1)
                    pool.wait_ge(k_step, p.upto())
                    G.tensor_tensor(k_sb[:], k_sb[:], k_relu[:], ALU.add).then_inc(k_ready, 1)
                if (i - 2).within(PAIRS):
                    rstd(mv2, ve2, rstd2, shift2, mv2_ready, rstd2_step, i - 2, 4)
                if (i - 4).within(PAIRS):
                    scatter(i - 4)

            pool.wait_ge(s_const, 16 * CONST_DMAS)
            pool.wait_ge(s_prep, 1)
            pool.wait_ge(s_posb, 2)
            pool.wait_ge(patches_ready, IMAGES // OCT)
            walk(pool, BEFORE_A, STEADY_A, AFTER_A, step)

            def store(t):
                k = t.slot(4)
                until, until2 = ahead(pool, t.upto()), ahead(pool, 16 * t.rounds(4, 4))
                pool.wait_ge(s_prep, 1)
                pool.wait_ge(result_ready, until)
                if t.had(4):
                    pool.wait_ge(stored[k], until2)
                G.tensor_copy(result_id[:, k:k + 1], rows_all[:, bass.ds(t.n, 1), ID].bitcast(I32)).then_inc(id_copied, 1)
                until = ahead(pool, t.upto())
                pool.wait_ge(s_prep, 1)
                pool.wait_ge(id_copied, until)
                G.indirect_dma_start(
                    out=out, out_offset=bass.IndirectOffsetOnAxis(ap=result_id[:, k:k + 1], axis=0),
                    in_=result[:, k, :], in_offset=None,
                    bounds_check=TOKENS - 1, oob_is_err=False).then_inc(stored[k], 16)

            walk(pool, BEFORE_B, STEADY_B, AFTER_B, lambda j: (j - 2).within(TILES) and store(j - 2))

        @block.scalar
        def _(act):
            S = nc.scalar
            act.dma_start(pos_s[:], pos).then_inc(s_small, 16)
            act.dma_start(tokb_s[:], tok_b).then_inc(s_small, 16)
            act.dma_start(cls_s[:], cls).then_inc(s_small, 16)
            act.dma_start(bq_s[:], bq).then_inc(s_small, 16)
            act.dma_start(gate_s[:], gate).then_inc(s_small, 16)
            for k, c in con.items():
                act.dma_start(c[:], consts[k]).then_inc(s_const, 16)
            act.dma_start(ids_s[:], ids).then_inc(s_const, 16)
            act.dma_start(wkv_raw, wkv).then_inc(s_weights, 16)
            act.dma_start(wq_raw, wq).then_inc(s_weights, 16)
            act.dma_start(wo_raw, wo).then_inc(s_weights, 16)
            act.dma_start(bias_row[0:1, 0:2 * D], bkv).then_inc(s_weights, 16)
            act.dma_start(bias_row[0:1, 2 * D:3 * D], bo).then_inc(s_weights, 16)

            def unit(u):
                k = u.slot(4)
                act.wait_ge(x_loaded[k], 16 * u.rounds(4))
                if u.had(2):
                    act.wait_ge(unit_done, u.upto(2))
                S.copy(xp_hi[:, u.slot(2)].rearrange("p f n -> p (f n)"), x_in[:, k * X_UNIT:(k + 1) * X_UNIT]).then_inc(x_hi_ready, 1)

            act.wait_ge(s_tokw, 32)
            S.copy(w_tok_hi[:].rearrange("p f d -> p (f d)"), w_tok_raw).then_inc(w_hi, 1)
            walk_units(act, unit)
            act.wait_ge(s_weights, 16 * WEIGHT_DMAS)
            S.copy(wkv_hi[:].rearrange("p k d -> p (k d)"), wkv_raw).then_inc(w_hi, 1)
            S.copy(wq_hi[:].rearrange("p k d -> p (k d)"), wq_raw).then_inc(w_hi, 1)
            S.copy(wo_hi[:].rearrange("p k d -> p (k d)"), wo_raw).then_inc(w_hi, 1)
            act.wait_ge(s_bias_chain, 6)
            for r in range(3):
                act.dma_start(bias3[r:r + 1, :], bias_part[:, r, :]).then_inc(s_bias_dma, 16)
            act.wait_ge(s_small, 16 * SMALL_DMAS)
            act.wait_ge(unit_done, UNITS)
            act.wait_ge(s_bias_dma, 48)

            def turned(bank):
                return bank[:, 0:4 * TOK].rearrange("p (k t) -> p k t", k=KC)

            def step(i):
                if (i - 4).within(PAIRS):
                    p = i - 4
                    act.wait_ge(top_ready, p.upto())
                    if p.had(2):
                        act.wait_ge(field_step, p.upto(2, 5))
                    S.activation(tanh_top[:, p.slot(2), :], top[:, p.slot(2), :], ACT.Tanh, scale=0.5).then_inc(tanh_ready, 1)
                if (i + 1).within(PAIRS):
                    p = i + 1
                    act.wait_ge(turn_done, p.upto())
                    if p.had(2):
                        act.wait_ge(q_done, p.upto(2))
                    S.copy(xnT_hi[:, p.slot(2), :, 0:2 * TOK], turned(b_turn)).then_inc(xnT_hi_ready, 1)
                if (i - 2).within(PAIRS):
                    p = i - 2
                    act.wait_ge(turn_attn_done, p.upto())
                    if p.had(1):
                        act.wait_ge(wo_done, p.upto(1))
                    S.copy(attnT_hi[:], turned(b_gate)).then_inc(attnT_hi_ready, 1)
                if (i - 3).within(PAIRS):
                    p = i - 3
                    k = p.slot(4)
                    act.wait_ge(rstd2_step, p.upto(0, 4))
                    if p.had(1):
                        act.wait_ge(turn2_done, p.upto(1))
                    for b in range(2):
                        last = S.activation(xn2[:, b, :], rows[:, k, b, 0:D], ACT.Identity,
                                            bias=shift2[:, k, b:b + 1], scale=rstd2[:, k, b:b + 1])
                    last.then_inc(xn2_ready, 1)
                if i.within(PAIRS):
                    p = i
                    act.wait_ge(kvp_done, p.upto())
                    if p.had(1):
                        act.wait_ge(k_ready, p.upto(1))
                        act.wait_ge(kvm_done, p.upto(1))
                    S.activation(k_exp[:], b_kvp[0:TOK, :, 0:D], ACT.Exp)
                    S.activation(k_relu[:], b_kvp[0:TOK, :, 0:D], ACT.Relu).then_inc(kv_parts, 1)
                    for b in range(2):
                        last = S.copy(v_sb[:, b, :, 0:P], b_kvp[0:TOK, b, D:2 * D].rearrange("p (k e) -> p k e", k=KC))
                    last.then_inc(v_ready, 1)
                if (i + 2).within(PAIRS):
                    p = i + 2
                    until, until2 = ahead(act, p.upto(0, 4)), ahead(act, p.upto(1))
                    act.wait_ge(s_small, 16)
                    act.wait_ge(rstd1_step, until)
                    if p.had(1):
                        act.wait_ge(turn_done, until2)
                    for b in range(2):
                        last = S.activation(xn[:, b, :], rows_all[0:TOK, bass.ds(2 * p.n + b, 1), 0:D], ACT.Identity,
                                            bias=shift1[:, p.slot(2), b:b + 1], scale=rstd1[:, p.slot(2), b:b + 1])
                    last.then_inc(xn_ready, 1)
                if (i - 3).within(PAIRS):
                    p = i - 3
                    act.wait_ge(turn2_done, p.upto())
                    if p.had(1):
                        act.wait_ge(gate_done, p.upto(1))
                    S.copy(xn2T[:], turned(b_turn)).then_inc(xn2T_ready, 1)
                if i.within(PAIRS):
                    p = i
                    act.wait_ge(q_done, p.upto())
                    if p.had(1):
                        act.wait_ge(q_ready, p.upto(1))
                    for c in range(KC):
                        at = b_qo[:, c * QW:c * QW + 2 * TOK]
                        S.activation(q_exp[:, c, :], at, ACT.Exp, bias=bq_s[:, c:c + 1])
                        last = S.activation(q_relu[:, c, :], at, ACT.Relu, bias=bq_s[:, c:c + 1])
                    last.then_inc(q_parts, 1)
                if (i + 3).within(PAIRS):
                    p = i + 3
                    until = ahead(act, p.upto())
                    act.wait_ge(s_small, 16)
                    act.wait_ge(back_done, until)
                    S.activation(rows_all[0:PATCHES + 1, bass.ds(2 * p.n, 2), 0:D],
                                 b_tok[0:PATCHES + 1, :].rearrange("p (b d) -> p b d", b=2), ACT.Copy).then_inc(h_ready, 1)
                e = i.n - FIRST_SPLIT if i.fixed else -1
                if 0 <= e < EXPERTS:
                    at = e * (GU + DOWN)
                    act.wait_ge(s_expert_w, 32 * EXPERTS)
                    act.wait_ge(back_done, PAIRS)
                    S.copy(wgu_hi[:, e].rearrange("p k d -> p (k d)"), expert_raw[:, at:at + GU])
                    S.copy(wdown_hi[:, e], expert_raw[:, at + GU:at + GU + DOWN]).then_inc(expert_hi, 1)

            walk(act, BEFORE_A, STEADY_A, AFTER_A, step)

            def tile_step(j):
                if (j + 2).within(TILES):
                    t = j + 2
                    act.wait_ge(turn_x_done, t.upto())
                    if t.had(4):
                        act.wait_ge(gu_done, t.upto(4))
                    S.copy(xsT_hi[:, t.slot(4)], b_tile(b_x, t, KC * P).rearrange("p (k t) -> p k t", k=KC)).then_inc(xsT_hi_ready, 1)
                if (j + 3).within(TILES):
                    t = j + 3
                    until, until2 = ahead(act, 16 * t.rounds(4)), ahead(act, t.upto(2))
                    act.wait_ge(s_small, 16)
                    act.wait_ge(row_loaded[t.slot(4)], until)
                    if t.had(2):
                        act.wait_ge(turn_x_done, until2)
                    at = rows_all[:, bass.ds(t.n, 1), :]
                    S.copy(affine[:, t.slot(4), :], at[:, :, SHIFT:GAIN + 1]).then_inc(affine_ready, 1)
                    act.wait_ge(affine_ready, t.upto())
                    S.activation(xs[:, t.slot(2)], at[:, :, 0:D], ACT.Identity,
                                 bias=affine[:, t.slot(4), 0:1], scale=affine[:, t.slot(4), 1:2]).then_inc(xs_ready, 1)
                if j.within(TILES):
                    t = j
                    act.wait_ge(gu_done, t.upto())
                    if t.had(2):
                        act.wait_ge(act_ready, t.upto(2))
                    S.activation(silu_g[:, t.slot(2)], b_tile(b_gu, t, INNER), ACT.Silu).then_inc(silu_ready, 1)
                if (j - 1).within(TILES):
                    t = j - 1
                    act.wait_ge(turn_a_done, t.upto())
                    if t.had(2):
                        act.wait_ge(down_done, t.upto(2))
                    S.copy(actT_hi[:, t.slot(2)], b_tile(b_a, t, P)).then_inc(actT_hi_ready, 1)

            walk(act, BEFORE_B, STEADY_B, AFTER_B, tile_step)

        @block.vector
        def _(dve):
            V = nc.vector

            def low(to, whole, high):
                return V.tensor_tensor(to, whole, high.bitcast(F32), ALU.subtract)

            V.memset(tail_rows[:, 0:ID], 0.0)
            V.memset(tail_rows[:, ID:].bitcast(I32), NO_TOKEN)
            V.memset(half_neg[:], -0.5)
            V.memset(ones_bf[:], 1.0)
            V.memset(bias3[:], 0.0).then_inc(s_prep, 1)
            dve.wait_ge(s_small, 16 * SMALL_DMAS)
            for c in range(KC):
                last = V.tensor_scalar(posb[:, c, :], pos_s[:, c, 1:], tokb_s[:, c:c + 1], None, ALU.add)
            last.then_inc(s_posb, 1)
            dve.wait_ge(s_const, 16 * CONST_DMAS)
            V.tensor_copy(earlier[:], con["c_earlier"][:])
            for k in range(2):
                last = V.tensor_copy(so_far[:, k], con["c_region"][:].rearrange("p (b e) -> p b e", b=2))
            last.then_inc(s_posb, 1)
            dve.wait_ge(w_hi, 1)
            low(w_tok_lo[:].rearrange("p f d -> p (f d)"), w_tok_raw, w_tok_hi[:].rearrange("p f d -> p (f d)")).then_inc(w_lo, 1)
            dve.wait_ge(s_posb, 2)

            def patches_out(q, k):
                dve.wait_ge(unit_done, 2 * q + 2)
                for c, bank in enumerate((b_kvp, b_att)):
                    last = V.tensor_tensor(
                        tokT_all[:, c, bass.ds(OCT * q, OCT), :],
                        bank[:, k, 0:OCT * PATCHES].rearrange("p (b n) -> p b n", b=OCT),
                        posb[:, c:c + 1, :].to_broadcast([P, OCT, PATCHES]), ALU.add)
                last.then_inc(patches_ready, 1)

            def unit(u):
                k = u.slot(4)
                dve.wait_ge(x_hi_ready, u.upto())
                low(xp_lo[:, u.slot(2)].rearrange("p f n -> p (f n)"), x_in[:, k * X_UNIT:(k + 1) * X_UNIT],
                    xp_hi[:, u.slot(2)].rearrange("p f n -> p (f n)")).then_inc(x_lo_ready, 1)
                if u.c % 2 == 0 and u.had(2):
                    patches_out(2 * u.m + u.c // 2 - 1, (u.c // 2 - 1) % 2)

            walk_units(dve, unit)
            dve.wait_ge(s_weights, 16 * WEIGHT_DMAS)
            left = bias_row
            for r in range(3):
                V.tensor_copy(bias_part[:, r, :], left[:]).then_inc(s_bias_chain, 1)
                dve.wait_ge(s_bias_chain, 2 * r + 1)
                V.tensor_tensor(bias_left[:], left[:], bias_part[:, r, :], ALU.subtract).then_inc(s_bias_chain, 1)
                dve.wait_ge(s_bias_chain, 2 * r + 2)
                left = bias_left
            dve.wait_ge(w_hi, 4)
            for lo, raw, hi in ((wkv_lo, wkv_raw, wkv_hi), (wq_lo, wq_raw, wq_hi), (wo_lo, wo_raw, wo_hi)):
                last = low(lo[:].rearrange("p k d -> p (k d)"), raw, hi[:].rearrange("p k d -> p (k d)"))
            last.then_inc(w_lo, 1)
            patches_out(UNITS // 2 - 1, (UNITS // 2 - 1) % 2)
            dve.wait_ge(s_bias_dma, 48)
            for c in range(KC):
                for b in range(2):
                    V.tensor_tensor(tokT[:, c, b, PATCHES:], pos_s[:, c, 0:1], cls_s[:, c:c + 1], ALU.add)
            for k in range(2):
                V.memset(xnT_hi[:, k, :, 2 * TOK:].bitcast(F32), 0.0)
                V.memset(xnT_lo[:, k, :, 2 * TOK:].bitcast(F32), 0.0)
            V.memset(v_sb[:, :, :, P:], 1.0)
            V.memset(rows[:, :, :, ID + 1:], 0.0).then_inc(room_ready, 1)

            def stats(src, to, mv, done, ready, p):
                for b in range(2):
                    last = V.bn_stats(to[:, b, :], src(b))
                last.then_inc(done, 1)
                until = ahead(dve, p.upto())
                dve.wait_ge(s_posb, 2)
                dve.wait_ge(done, until)
                for b in range(2):
                    last = V.bn_aggr(mv[:, b, :], to[:, b, :])
                last.then_inc(ready, 1)

            def turned(bank):
                return bank[:, 0:4 * TOK].rearrange("p (k t) -> p k t", k=KC)

            def step(i):
                if (i - 4).within(PAIRS):
                    p = i - 4
                    dve.wait_ge(gate_done, p.upto())
                    if p.had(2):
                        dve.wait_ge(tanh_ready, p.upto(2))
                    logits = b_gate[0:TOK, 0:2 * EXPERTS].rearrange("p (b e) -> p b e", b=2)
                    V.tensor_reduce(top[:, p.slot(2), :], logits, AX_X, ALU.max).then_inc(top_ready, 1)
                    dve.wait_ge(top_ready, p.upto())
                    for b in range(2):
                        last = V.scalar_tensor_tensor(ranked[:, b, :], logits[:, b, :], top[:, p.slot(2), b:b + 1],
                                                      con["c_weight8"][:], ALU.is_equal, ALU.mult)
                    last.then_inc(ranked_ready, 1)
                if (i - 1).within(PAIRS):
                    p = i - 1
                    dve.wait_ge(kvm_done, p.upto())
                    if p.had(1):
                        dve.wait_ge(apply_done, p.upto(1))
                    V.tensor_tensor(kv_sb[:].rearrange("p b k w -> p (b k) w"),
                                    b_att[:, :, 0:KC * KVW].rearrange("p b (k w) -> p b k w", k=KC),
                                    mask[:].rearrange("p (a w) -> p a w", a=1).to_broadcast([P, 2 * KC, KVW]),
                                    ALU.mult).then_inc(kv_ready, 1)
                    dve.wait_ge(q_parts, p.upto())
                    V.scalar_tensor_tensor(qT[:], q_exp[:], 1.0, q_relu[:], ALU.min, ALU.add).then_inc(q_ready, 1)
                if (i + 1).within(PAIRS):
                    p = i + 1
                    dve.wait_ge(xnT_hi_ready, p.upto())
                    low(xnT_lo[:, p.slot(2), :, 0:2 * TOK], turned(b_turn), xnT_hi[:, p.slot(2), :, 0:2 * TOK]).then_inc(xnT_lo_ready, 1)
                if (i - 2).within(PAIRS):
                    p = i - 2
                    dve.wait_ge(attnT_hi_ready, p.upto())
                    low(attnT_lo[:], turned(b_gate), attnT_hi[:]).then_inc(attnT_lo_ready, 1)
                if (i - 4).within(PAIRS):
                    p = i - 4
                    dve.wait_ge(ranked_ready, p.upto())
                    V.tensor_reduce(first[:], ranked[:], AX_X, ALU.max).then_inc(first_ready, 1)
                    dve.wait_ge(first_ready, p.upto())
                    if p.had(2):
                        dve.wait_ge(so_far_ready, p.upto(2))
                        dve.wait_ge(rank_done, p.upto(2))
                    V.tensor_tensor(chosen[:, p.slot(2)], ranked[:],
                                    first[:].rearrange("p (b a) -> p b a", a=1).to_broadcast([TOK, 2, EXPERTS]),
                                    ALU.is_equal).then_inc(chosen_ready, 1)
                if (i + 2).within(PAIRS):
                    p = i + 2
                    until, until2, until3 = ahead(dve, p.upto()), ahead(dve, 16 * p.rounds(2)), ahead(dve, p.upto(2))
                    dve.wait_ge(s_posb, 2)
                    dve.wait_ge(h_ready, until)
                    dve.wait_ge(s_in[p.slot(2)], until2)
                    if p.had(2):
                        dve.wait_ge(xn_ready, until3)
                    stats(lambda b: rows_all[0:TOK, bass.ds(2 * p.n + b, 1), 0:D], stats1, mv1[:, p.slot(2)],
                          stats1_done, mv1_ready, p)
                if (i - 2).within(PAIRS):
                    p = i - 2
                    k = p.slot(4)
                    dve.wait_ge(wo_done, p.upto())
                    if p.had(4):
                        dve.wait_ge(scattered[k], 32 * p.rounds(4, 4))
                    V.tensor_tensor(rows[:, k, :, 0:D], b_qo[0:TOK, 0:2 * D].rearrange("p (b d) -> p b d", b=2),
                                    rows_all[0:TOK, bass.ds(2 * p.n, 2), 0:D], ALU.add).then_inc(h2_ready, 1)
                    until = ahead(dve, p.upto())
                    dve.wait_ge(s_posb, 2)
                    dve.wait_ge(h2_ready, until)
                    stats(lambda b: rows[:, k, b, 0:D], stats2, mv2[:, k], stats2_done, mv2_ready, p)
                if (i - 1).within(PAIRS):
                    p = i - 1
                    dve.wait_ge(apply_done, p.upto())
                    heads = b_att[0:TOK, :, 0:KC * KVW].rearrange("p b (k w) -> p b k w", k=KC)
                    V.tensor_scalar(den[:].rearrange("p b (k h) -> p b k h", k=KC), heads[:, :, :, P:KVW],
                                    Z_EPS, None, ALU.add).then_inc(den_done, 1)
                    dve.wait_ge(den_done, p.upto())
                    V.reciprocal(z[:], den[:]).then_inc(z_done, 1)
                    dve.wait_ge(z_done, p.upto())
                    if p.had(1):
                        dve.wait_ge(turn_attn_done, p.upto(1))
                    for b in range(2):
                        last = V.tensor_tensor(
                            attn[:, b, :].rearrange("p (k h e) -> p k h e", k=KC, h=HPC),
                            heads[:, b, :, 0:P].rearrange("p k (h e) -> p k h e", h=HPC),
                            z[:, b, :].rearrange("p (k h a) -> p k h a", k=KC, a=1).to_broadcast([TOK, KC, HPC, DH]),
                            ALU.mult)
                    last.then_inc(attn_ready, 1)
                if (i - 4).within(PAIRS):
                    p = i - 4
                    dve.wait_ge(rank_done, p.upto())
                    for b in range(2):
                        last = V.tensor_tensor_reduce(place_e[:, b, :], b_tok[0:TOK, b * EXPERTS:(b + 1) * EXPERTS],
                                                      chosen[:, p.slot(2), b, :], 1.0, 0.0, ALU.mult, ALU.add,
                                                      place_f[:, p.slot(4), b:b + 1])
                    last.then_inc(place_ready, 1)
                e = i.n - FIRST_SPLIT if i.fixed else -1
                if 0 <= e < EXPERTS:
                    at = e * (GU + DOWN)
                    dve.wait_ge(expert_hi, e + 1)
                    low(wgu_lo[:, e].rearrange("p k d -> p (k d)"), expert_raw[:, at:at + GU], wgu_hi[:, e].rearrange("p k d -> p (k d)"))
                    low(wdown_lo[:, e], expert_raw[:, at + GU:at + GU + DOWN], wdown_hi[:, e]).then_inc(expert_lo, 1)

            walk(dve, BEFORE_A, STEADY_A, AFTER_A, step)

            done = [0]

            def link(ins):
                ins.then_inc(table_step, 1)
                done[0] += 1
                dve.wait_ge(table_step, done[0])

            dve.wait_ge(table_pe, 1)
            link(V.tensor_copy(row_end[:], b_tok[0:EXPERTS, 0:1]))
            link(V.tensor_scalar(held[:], row_end[:], con["c_regcol"][:, 0:1], float(P - 1), ALU.subtract, ALU.add))
            link(V.tensor_copy(held_i[:], held[:]))
            link(V.tensor_scalar(tiles_i[:], held_i[:], P.bit_length() - 1, None, ALU.logical_shift_right))
            link(V.tensor_copy(tiles_f[:], tiles_i[:]))
            dve.wait_ge(table_pe, 2)
            V.tensor_copy(tail_at[:], b_turn[0:1, 2 * EXPERTS:3 * EXPERTS]).then_inc(table_ready, 1)
            link(V.tensor_copy(ends[:], b_turn[0:1, 0:2 * EXPERTS]))

            def over_slots(ap):
                return ap.rearrange("p (a e) -> p a e", a=1).to_broadcast([1, TILES, EXPERTS])

            link(V.tensor_tensor(past[:], con["c_slot"][:].rearrange("p (t e) -> p t e", t=TILES),
                                 over_slots(ends[:, 0:EXPERTS]), ALU.is_ge))
            link(V.tensor_reduce(slot_e[:], past[:], AX_X, ALU.add))
            link(V.tensor_tensor(past_n[:], past[:], over_slots(ends[:, EXPERTS:]), ALU.mult))
            link(V.tensor_reduce(slot_s[:], past_n[:], AX_X, ALU.add))
            link(V.scalar_tensor_tensor(slot_r[:], slot_s[:], -float(P), con["c_slotrow"][:], ALU.mult, ALU.add))
            link(V.scalar_tensor_tensor(slot_r2[:], slot_e[:], float(REGION), slot_r[:], ALU.mult, ALU.add))
            V.tensor_scalar(slot_expert[:], slot_e[:], float(EXPERTS - 1), None, ALU.min)
            V.tensor_scalar(slot_row[:], slot_r2[:], float(EXPERTS * REGION), None, ALU.min).then_inc(table_ready, 1)

            def tile_step(j):
                if (j + 2).within(TILES):
                    t = j + 2
                    dve.wait_ge(xsT_hi_ready, t.upto())
                    low(xsT_lo[:, t.slot(4)], b_tile(b_x, t, KC * P).rearrange("p (k t) -> p k t", k=KC),
                        xsT_hi[:, t.slot(4)]).then_inc(xsT_lo_ready, 1)
                if j.within(TILES):
                    t = j
                    dve.wait_ge(silu_ready, t.upto())
                    if t.had(2):
                        dve.wait_ge(turn_a_done, t.upto(2))
                    V.tensor_tensor(act_u[:, t.slot(2)], b_tile(b_gu, t, INNER, INNER), silu_g[:, t.slot(2)],
                                    ALU.mult).then_inc(act_ready, 1)
                if (j - 1).within(TILES):
                    t = j - 1
                    dve.wait_ge(actT_hi_ready, t.upto())
                    low(actT_lo[:, t.slot(2)], b_tile(b_a, t, P), actT_hi[:, t.slot(2)]).then_inc(actT_lo_ready, 1)
                if (j - 2).within(TILES):
                    t = j - 2
                    dve.wait_ge(down_done, t.upto())
                    if t.had(4):
                        dve.wait_ge(stored[t.slot(4)], 16 * t.rounds(4, 4))
                    V.tensor_tensor(result[:, t.slot(4)], b_tile(b_y, t, D), rows_all[:, bass.ds(t.n, 1), 0:D],
                                    ALU.add).then_inc(result_ready, 1)

            walk(dve, BEFORE_B, STEADY_B, AFTER_B, tile_step)

        @block.tensor
        def _(pe):
            T = nc.tensor

            def product(to, left, right, start, stop):
                (left_hi, left_lo), (right_hi, right_lo) = left, right
                T.matmul(to, left_hi, right_hi, start=start, stop=False)
                T.matmul(to, left_hi, right_lo, start=False, stop=False)
                return T.matmul(to, left_lo, right_hi, start=False, stop=stop)

            def unit(u):
                pe.wait_ge(x_lo_ready, u.upto())
                if u.c % 2 == 0 and u.had(4):
                    pe.wait_ge(patches_ready, 2 * u.m + u.c // 2 - 1)
                for c, bank in enumerate((b_kvp, b_att)):
                    for k in range(FC // 2):
                        f = (u.c % 2) * (FC // 2) + k
                        w, xk = slice(c * P, (c + 1) * P), u.slot(2)
                        last = product(bank[:, (u.c // 2) % 2, 0:OCT * PATCHES], (w_tok_hi[:, f, w], w_tok_lo[:, f, w]),
                                       (xp_hi[:, xk, k, :], xp_lo[:, xk, k, :]), f == 0, f == FC - 1)
                last.then_inc(unit_done, 1)

            pe.wait_ge(w_lo, 1)
            walk_units(pe, unit)

            def step(i):
                if (i - 1).within(PAIRS):
                    p = i - 1
                    pe.wait_ge(k_ready, p.upto())
                    pe.wait_ge(v_ready, p.upto())
                    if p.had(1):
                        pe.wait_ge(attn_ready, p.upto(1))
                    for b in range(2):
                        for c in range(KC):
                            last = T.matmul(b_att[:, b, c * KVW:(c + 1) * KVW], k_sb[:, b, c * P:(c + 1) * P],
                                            v_sb[:, b, c, :], start=True, stop=True)
                    last.then_inc(kvm_done, 1)
                if (i + 1).within(PAIRS):
                    p = i + 1
                    pe.wait_ge(xn_ready, p.upto())
                    if p.had(5):
                        pe.wait_ge(xn2T_ready, p.upto(5))
                    elif p.had(1):
                        pe.wait_ge(xnT_lo_ready, p.upto(1))
                    for k in range(KC):
                        for b in range(2):
                            at = (2 * k + b) * TOK
                            last = T.transpose(b_turn[:, at:at + TOK], xn[:, b, k * P:(k + 1) * P], ident[0:TOK, 0:TOK])
                    last.then_inc(turn_done, 1)
                if (i - 2).within(PAIRS):
                    p = i - 2
                    pe.wait_ge(attn_ready, p.upto())
                    if p.had(2):
                        pe.wait_ge(ranked_ready, p.upto(2))
                    elif p.had(1):
                        pe.wait_ge(attnT_lo_ready, p.upto(1))
                    for c in range(KC):
                        for b in range(2):
                            at = (2 * c + b) * TOK
                            last = T.transpose(b_gate[:, at:at + TOK], attn[:, b, c * P:(c + 1) * P], ident[0:TOK, 0:TOK])
                    last.then_inc(turn_attn_done, 1)
                if i.within(PAIRS):
                    p = i
                    pe.wait_ge(xnT_lo_ready, p.upto())
                    if p.had(1):
                        pe.wait_ge(v_ready, p.upto(1))
                    for b in range(2):
                        T.matmul(b_kvp[0:TOK, b, :], ones_bf[:, :], bias3[:, 0:2 * D], start=True, stop=False)
                        for k in range(KC):
                            at = slice(b * TOK, (b + 1) * TOK)
                            last = product(b_kvp[0:TOK, b, :], (xnT_hi[:, p.slot(2), k, at], xnT_lo[:, p.slot(2), k, at]),
                                           (wkv_hi[:, k, :], wkv_lo[:, k, :]), False, k == KC - 1)
                    last.then_inc(kvp_done, 1)
                if (i - 2).within(PAIRS):
                    p = i - 2
                    pe.wait_ge(attnT_lo_ready, p.upto())
                    if (p + 1).within(PAIRS):
                        pe.wait_ge(q_parts, p.upto(-1))
                    else:
                        pe.wait_ge(h2_ready, p.upto(1))
                    for b in range(2):
                        to = b_qo[0:TOK, b * D:(b + 1) * D]
                        T.matmul(to, ones_bf[:, :], bias3[:, 2 * D:3 * D], start=True, stop=False)
                        for c in range(KC):
                            at = slice(b * TOK, (b + 1) * TOK)
                            last = product(to, (attnT_hi[:, c, at], attnT_lo[:, c, at]), (wo_hi[:, c, :], wo_lo[:, c, :]),
                                           False, c == KC - 1)
                    last.then_inc(wo_done, 1)
                if (i - 1).within(PAIRS):
                    p = i - 1
                    pe.wait_ge(kv_ready, p.upto())
                    pe.wait_ge(q_ready, p.upto())
                    for b in range(2):
                        for c in range(KC):
                            last = T.matmul(b_att[0:TOK, b, c * KVW:(c + 1) * KVW], qT[:, c, b * TOK:(b + 1) * TOK],
                                            kv_sb[:, b, c, :], start=True, stop=True)
                    last.then_inc(apply_done, 1)
                if (i - 4).within(PAIRS):
                    p = i - 4
                    pe.wait_ge(chosen_ready, p.upto())
                    if p.had(1):
                        pe.wait_ge(so_far_ready, p.upto(1))
                    if (p + 6).within(PAIRS):
                        pe.wait_ge(h_ready, p.upto(-6))
                    else:
                        pe.wait_ge(place_ready, p.upto(1))
                    ranks, second = b_tok[0:TOK, 0:2 * EXPERTS], b_tok[0:TOK, EXPERTS:2 * EXPERTS]
                    T.matmul(ranks, earlier[:], chosen[:, p.slot(2)].rearrange("p b e -> p (b e)"), start=True, stop=False)
                    T.matmul(second, ones_bf[0:TOK, :], chosen[:, p.slot(2), 0, :], start=False, stop=False)
                    for b in range(2):
                        last = T.matmul(ranks, ones_bf[:, :], so_far[:, p.slot(2), b:b + 1, :].to_broadcast([P, 2, EXPERTS]),
                                        start=False, stop=(b == 1))
                    last.then_inc(rank_done, 1)
                if (i - 3).within(PAIRS):
                    p = i - 3
                    pe.wait_ge(xn2_ready, p.upto())
                    if (p + 4).within(PAIRS):
                        pe.wait_ge(xnT_lo_ready, p.upto(-4))
                    else:
                        pe.wait_ge(xn2T_ready, p.upto(1))
                    for k in range(KC):
                        for b in range(2):
                            at = (2 * k + b) * TOK
                            last = T.transpose(b_turn[:, at:at + TOK], xn2[:, b, k * P:(k + 1) * P], ident[0:TOK, 0:TOK])
                    last.then_inc(turn2_done, 1)
                if i.within(PAIRS):
                    p = i
                    if p.had(2):
                        pe.wait_ge(h2_ready, p.upto(2))
                    elif p.had(1):
                        pe.wait_ge(q_parts, p.upto(1))
                    for c in range(KC):
                        for k in range(KC):
                            w = slice(c * P, (c + 1) * P)
                            last = product(b_qo[:, c * QW:(c + 1) * QW], (wq_hi[:, k, w], wq_lo[:, k, w]),
                                           (xnT_hi[:, p.slot(2), k, :], xnT_lo[:, p.slot(2), k, :]), k == 0, k == KC - 1)
                    last.then_inc(q_done, 1)
                if (i + 3).within(PAIRS):
                    p = i + 3
                    until, until2 = ahead(pe, p.upto()), ahead(pe, p.upto(7 if p.had(7) else 1))
                    pe.wait_ge(w_lo, 2)
                    pe.wait_ge(tokT_ready, until)
                    if p.had(7):
                        pe.wait_ge(place_ready, until2)
                    elif p.had(1):
                        pe.wait_ge(h_ready, until2)
                    for b in range(2):
                        for c in range(KC):
                            at = b * D + c * P
                            last = T.transpose(b_tok[0:PATCHES + 1, at:at + P], tokT[:, c, b, :], ident[:])
                    last.then_inc(back_done, 1)
                if (i - 3).within(PAIRS):
                    p = i - 3
                    pe.wait_ge(xn2T_ready, p.upto())
                    if (p + 1).within(PAIRS):
                        pe.wait_ge(attnT_lo_ready, p.upto(-1))
                    else:
                        pe.wait_ge(ranked_ready, p.upto(1))
                    for b in range(2):
                        for k in range(KC):
                            last = T.matmul(b_gate[0:TOK, b * EXPERTS:(b + 1) * EXPERTS], xn2T[:, k, b * TOK:(b + 1) * TOK],
                                            gate_s[:, k, :], start=(k == 0), stop=(k == KC - 1))
                    last.then_inc(gate_done, 1)

            pe.wait_ge(s_const, 16 * CONST_DMAS)
            pe.wait_ge(s_posb, 2)
            pe.wait_ge(w_lo, 2)
            pe.wait_ge(s_bias_dma, 48)
            pe.wait_ge(room_ready, 1)
            walk(pe, BEFORE_A, STEADY_A, AFTER_A, step)

            pe.wait_ge(place_ready, PAIRS)
            pe.wait_ge(so_far_ready, PAIRS)
            for k in range(4):
                pe.wait_ge(scattered[k], 2 * 16 * PAIRS // 4)
            for b in range(2):
                last = T.matmul(b_tok[0:EXPERTS, 0:2], so_far[:, PAIRS % 2, b, :], ones_bf[:, 0:2], start=(b == 0), stop=(b == 1))
            last.then_inc(table_pe, 1)
            pe.wait_ge(table_step, 5)
            T.matmul(b_turn[0:1, 0:2 * EXPERTS], tiles_f[:], con["c_tri"][:], start=True, stop=True)
            T.matmul(b_turn[0:1, 2 * EXPERTS:3 * EXPERTS], row_end[:], ident[0:EXPERTS, 0:EXPERTS],
                     start=True, stop=True).then_inc(table_pe, 1)
            pe.wait_ge(table_ready, 2)
            pe.wait_ge(expert_lo, EXPERTS)
            expert_of = [pe.alloc_register(f"expert{k}") for k in range(4)]
            pe.reg_load(expert_of[0], slot_expert[0:1, 0:1])

            def expert(t):
                return pe.snap(expert_of[t.slot(4)], min_val=0, max_val=EXPERTS - 1)

            def tile_step(j):
                if (j + 2).within(TILES):
                    t = j + 2
                    pe.wait_ge(xs_ready, t.upto())
                    if t.had(2):
                        pe.wait_ge(xsT_lo_ready, t.upto(2))
                    for k in range(KC):
                        last = T.transpose(b_tile(b_x, t, P, k * P), xs[:, t.slot(2), k * P:(k + 1) * P], ident[:])
                    last.then_inc(turn_x_done, 1)
                if j.within(TILES):
                    t = j
                    e = expert(t)
                    pe.wait_ge(xsT_lo_ready, t.upto())
                    if t.had(2):
                        pe.wait_ge(act_ready, t.upto(2))
                    for k in range(KC):
                        last = product(b_tile(b_gu, t, 2 * INNER), (xsT_hi[:, t.slot(4), k, :], xsT_lo[:, t.slot(4), k, :]),
                                       (wgu_hi[:, bass.ds(e, 1), k, :], wgu_lo[:, bass.ds(e, 1), k, :]), k == 0, k == KC - 1)
                    last.then_inc(gu_done, 1)
                    if (t + 1).within(TILES):
                        pe.reg_load(expert_of[(t + 1).slot(4)], slot_expert[0:1, bass.ds((t + 1).n, 1)])
                if (j - 1).within(TILES):
                    t = j - 1
                    pe.wait_ge(act_ready, t.upto())
                    if t.had(2):
                        pe.wait_ge(actT_lo_ready, t.upto(2))
                    T.transpose(b_tile(b_a, t, P), act_u[:, t.slot(2)], ident[:]).then_inc(turn_a_done, 1)
                if (j - 2).within(TILES):
                    t = j - 2
                    e = expert(t)
                    pe.wait_ge(actT_lo_ready, t.upto())
                    if t.had(2):
                        pe.wait_ge(result_ready, t.upto(2))
                    product(b_tile(b_y, t, D), (actT_hi[:, t.slot(2)], actT_lo[:, t.slot(2)]),
                            (wdown_hi[:, bass.ds(e, 1), :], wdown_lo[:, bass.ds(e, 1), :]), True, True).then_inc(down_done, 1)

            walk(pe, BEFORE_B, STEADY_B, AFTER_B, tile_step)


def constants():
    f = np.float32
    d, h = np.arange(P), np.arange(HPC)
    own = (d[:, None] // DH == h[None, :]).astype(f)
    e = np.arange(EXPERTS)
    t = np.arange(TILES)
    region = np.zeros((P, 2 * EXPERTS), f)
    region[TOK, 0:EXPERTS] = e * REGION
    return {
        "c_ident": np.eye(P, dtype=f),
        "c_earlier": np.triu(np.ones((TOK, TOK), f), 1),
        "c_mask": np.concatenate([np.repeat(own, DH, axis=1), own], axis=1),
        "c_weight8": np.tile((EXPERTS - e).astype(f), (TOK, 1)),
        "c_region": region,
        "c_regcol": (e * REGION).astype(f)[:, None],
        "c_tri": np.concatenate([np.triu(np.ones((EXPERTS, EXPERTS), f)), np.eye(EXPERTS, dtype=f)], axis=1),
        "c_slot": np.repeat(t, EXPERTS).astype(f)[None],
        "c_slotrow": (t * P).astype(f)[None],
    }


def token_ids():
    at = np.concatenate([np.arange(1, PATCHES + 1), [0], np.arange(PATCHES + 1, TOK)])
    return (np.arange(IMAGES)[None, :] * TOK + at[:, None]).astype(np.int32)


def kernel(**inputs):
    import numpy as _np
    import concourse.bacc as _bacc
    from concourse import mybir as _mybir
    from concourse.bass_utils import run_bass_kernel_spmd as _run

    v = {k.replace("L0_", ""): _np.asarray(a) for k, a in inputs.items()}

    def chunks(a):
        return a.reshape(-1, P, a.shape[-1]).transpose(1, 0, 2)

    px = 16
    patches = v["x"].reshape(IMAGES // OCT, OCT, 3, 6, px, 6, px).transpose(0, 2, 4, 6, 1, 3, 5)
    layout = {
        "x": patches.reshape(IMAGES // OCT, 2, FC // 2, P, OCT * PATCHES).transpose(0, 1, 3, 2, 4)
             .reshape(2 * IMAGES // OCT, P, -1),
        "txt": v["txt"].transpose(1, 0, 2),
        "w_tok": chunks(v["tok_W"].T).reshape(P, -1),
        "pos": chunks(v["tok_pos_enc"][0].T),
        "tok_b": v["tok_b"].reshape(KC, P).T,
        "cls": v["tok_cls_token"].reshape(KC, P).T,
        "wq": chunks(v["attn_Wq"].T).reshape(P, -1),
        "bq": v["attn_bq"].reshape(KC, P).T,
        "wkv": chunks(_np.concatenate([v["attn_Wk"].T, v["attn_Wv"].T], axis=1)).reshape(P, -1),
        "bkv": _np.concatenate([v["attn_bk"], v["attn_bv"]])[None],
        "wo": chunks(v["attn_Wo"].T).reshape(P, -1),
        "bo": v["attn_bo"][None],
        "gate": chunks(v["ffn_gate_w"].T),
        "wgu": _np.concatenate([v["ffn_w_gate"], v["ffn_w_up"]], axis=1).transpose(2, 0, 1)
               .reshape(KC, P, EXPERTS, 2 * INNER).transpose(1, 2, 0, 3).reshape(P, -1),
        "wdown": v["ffn_w_down"].transpose(2, 0, 1).reshape(P, -1),
        "ids": token_ids(),
    }
    layout.update(constants())
    nc = _bacc.Bacc("TRN2", target_bir_lowering=False, num_devices=1)
    arrays, args = {}, {}
    for name, a in layout.items():
        a = _np.ascontiguousarray(a)
        arrays[f"in_{name}"] = a
        args[name] = nc.dram_tensor(f"in_{name}", a.shape, _mybir.dt.from_np(a.dtype), kind="ExternalInput").ap()
    out = nc.dram_tensor("out_0", (TOKENS, D), _mybir.dt.float32, kind="ExternalOutput").ap()
    consts = {k: args.pop(k) for k in CONSTS}
    build(nc, consts=consts, out=out, **args)
    r = _run(nc, [arrays], core_ids=[0])
    return r.results[0]["out_0"].reshape(IMAGES, TOK, D)
```

```python
from contextlib import ExitStack

import numpy as np

import concourse.bass as bass
from concourse import mybir

F32 = mybir.dt.float32
F32R = mybir.dt.float32r
BF16 = mybir.dt.bfloat16
I32 = mybir.dt.int32
U32 = mybir.dt.uint32
ALU = mybir.AluOpType
ACT = mybir.ActivationFunctionType
AX_X = mybir.AxisListType.X

P = 128
IMAGES = 64
PAIRS = IMAGES // 2
PATCHES = 36
CLS_AT = PATCHES
TXT = 77
TOK = PATCHES + 1 + TXT
TOKENS = IMAGES * TOK
D = 256
KC = D // P
FEAT = 768
FC = FEAT // P
HEADS = 16
DH = D // HEADS
HPC = P // DH
KVW = P + HPC
EXPERTS = 8
INNER = 128
REGION = TOKENS + P
ROW = D + 4
SHIFT, GAIN, ID = D, D + 1, D + 2
OCT = 8
QW = 256
TILES = (TOKENS + EXPERTS * (P - 1)) // P
NO_TOKEN = 1 << 20
LN_EPS = 1e-5
Z_EPS = 1e-6

CONSTS = {
    "c_ident": (P, P), "c_earlier": (TOK, TOK), "c_mask": (P, KVW), "c_weight8": (TOK, EXPERTS),
    "c_region": (P, 2 * EXPERTS), "c_regcol": (EXPERTS, 1), "c_tri": (EXPERTS, 2 * EXPERTS),
    "c_slot": (1, TILES * EXPERTS), "c_slotrow": (1, TILES),
}
CONST_W = sum(w for _, w in CONSTS.values())


class Turn:

    def __init__(self, m, c, unroll=4):
        self.m, self.c, self.unroll, self.fixed = m, c, unroll, isinstance(m, int)
        self.n = unroll * m + c

    def __add__(self, k):
        return Turn(self.m, self.c + k, self.unroll)

    def __sub__(self, k):
        return Turn(self.m, self.c - k, self.unroll)

    def had(self, back):
        return not self.fixed or self.n - back >= 0

    def within(self, count):
        return not self.fixed or 0 <= self.n < count

    def upto(self, back=0, per=1):
        return per * (self.n - back + 1)

    def slot(self, ring):
        return self.c % ring

    def rounds(self, ring, back=0):
        return self.m * (self.unroll // ring) + (self.c - back) // ring + 1


def build(nc, x, txt, w_tok, pos, tok_b, cls, wq, bq, wkv, bkv, wo, bo, gate, wgu, wdown, ids, consts, out):
    scratch = nc.dram_tensor("sorted_rows", (EXPERTS * REGION + P, ROW), F32, kind="Internal").ap()

    with ExitStack() as ctx:
        def sb(name, shape, dt=F32, at=ctx):
            return at.enter_context(nc.sbuf_tensor(name, shape, dt))

        def parts(name, shape, at=ctx):
            return sb(name + "_hi", shape, F32R, at), sb(name + "_lo", shape, F32R, at)

        def ps(name, shape):
            return ctx.enter_context(nc.psum_tensor(name, shape, F32))

        def sem(name):
            return ctx.enter_context(nc.semaphore(name))

        rows_all = sb("rows_all", [P, TILES, ROW])
        wq_hi, wq_lo = parts("wq", [P, KC, D])
        wkv_hi, wkv_lo = parts("wkv", [P, KC, 2 * D])
        wo_hi, wo_lo = parts("wo", [P, KC, D])
        wgu_hi, wgu_lo = parts("wgu", [P, EXPERTS, KC, 2 * INNER])
        gate_s = sb("gate_s", [P, KC, EXPERTS])
        bq_s = sb("bq_s", [P, KC])
        tokb_s = sb("tokb_s", [P, KC])
        cls_s = sb("cls_s", [P, KC])
        pos_s = sb("pos_s", [P, KC, PATCHES + 1])
        posb = sb("posb", [P, KC, PATCHES])
        bkv_s = sb("bkv_s", [TOK, 2 * D])
        bias3 = sb("bias3", [P, D], BF16)
        ones_bf = sb("ones_bf", [P, TOK], BF16)
        earlier = sb("earlier", [TOK, TOK], BF16)
        half_neg = sb("half_neg", [P, 2])
        silu_ahead = sb("silu_ahead", [P, 1])
        ids_s = sb("ids_s", [TOK, IMAGES], I32)
        tail_rows = sb("tail_rows", [P, ROW])
        con_s = sb("con_s", [P, CONST_W])
        con, at = {}, 0
        for name, (height, width) in CONSTS.items():
            con[name] = con_s[0:height, at:at + width]
            at += width
        ident, mask = con["c_ident"], con["c_mask"]
        so_far = sb("so_far", [P, 2, 2, EXPERTS], BF16)

        with ExitStack() as early:
            tokT_all = sb("tokT_all", [P, KC, IMAGES, PATCHES], at=early)
        wdown_hi, wdown_lo = parts("wdown", [P, EXPERTS, D])
        sb("wdown_rest", [P, KC * IMAGES * PATCHES - 2 * EXPERTS * D])

        tokT = sb("tokT", [P, KC, 2, PATCHES + 1])
        stats1 = sb("stats1", [TOK, 2, 6])
        mv1 = sb("mv1", [TOK, 2, 2, 2])
        ve1 = sb("ve1", [TOK, 2, 2])
        rstd1 = sb("rstd1", [TOK, 2, 2])
        shift1 = sb("shift1", [TOK, 2, 2])
        xn = sb("xn", [TOK, 2, D])
        xnT_hi, xnT_lo = parts("xnT", [P, 2, KC, QW])

        held = sb("held", [EXPERTS, 1])
        held_i = sb("held_i", [EXPERTS, 1], I32)
        tiles_i = sb("tiles_i", [EXPERTS, 1], I32)
        tiles_f = sb("tiles_f", [EXPERTS, 1])
        ends = sb("ends", [1, 2 * EXPERTS])
        tail_at = sb("tail_at", [1, EXPERTS], I32)
        past = sb("past", [1, TILES, EXPERTS])
        past_n = sb("past_n", [1, TILES, EXPERTS])
        slot_e = sb("slot_e", [1, TILES])
        slot_s = sb("slot_s", [1, TILES])
        slot_r = sb("slot_r", [1, TILES])
        slot_r2 = sb("slot_r2", [1, TILES])
        slot_row = sb("slot_row", [1, TILES], I32)
        slot_expert = sb("slot_expert", [1, TILES], I32)

        with ExitStack() as room:
            xp_hi, xp_lo = parts("xp", [P, 2, FC // 2, OCT * PATCHES], room)
            w_tok_hi, w_tok_lo = parts("w_tok", [P, FC, D], room)
            bias_row = sb("bias_row", [1, D], at=room)
            bias_left = sb("bias_left", [1, D], at=room)
            bias_part = sb("bias_part", [1, 3, D], BF16, room)

        with ExitStack() as room:
            q_exp = sb("q_exp", [P, KC, 2 * TOK], at=room)
            q_relu = sb("q_relu", [P, KC, 2 * TOK], at=room)
            qT = sb("qT", [P, KC, 2 * TOK], at=room)
            k_in = sb("k_in", [TOK, 2, D], at=room)
            k_neg = sb("k_neg", [TOK, 2, D], at=room)
            k_exp = sb("k_exp", [TOK, 2, D], at=room)
            k_relu = sb("k_relu", [TOK, 2, D], at=room)
            k_sb = sb("k_sb", [TOK, 2, D], at=room)
            v_sb = sb("v_sb", [TOK, 2, KC, KVW], at=room)
            kv_sb = sb("kv_sb", [P, 2, KC, KVW], at=room)
            den = sb("den", [TOK, 2, HEADS], at=room)
            z = sb("z", [TOK, 2, HEADS], at=room)
            attn = sb("attn", [TOK, 2, D], at=room)
            attnT_hi, attnT_lo = parts("attnT", [P, KC, 2 * TOK], room)
            rows = sb("rows", [TOK, 4, 2, ROW], at=room)
            stats2 = sb("stats2", [TOK, 2, 6], at=room)
            mv2 = sb("mv2", [TOK, 4, 2, 2], at=room)
            ve2 = sb("ve2", [TOK, 2, 2], at=room)
            rstd2 = sb("rstd2", [TOK, 4, 2], at=room)
            shift2 = sb("shift2", [TOK, 4, 2], at=room)
            xn2 = sb("xn2", [TOK, 2, D], at=room)
            xn2T = sb("xn2T", [P, KC, 2 * TOK], at=room)
            top = sb("top", [TOK, 2, 2], at=room)
            ranked = sb("ranked", [TOK, 2, EXPERTS], at=room)
            first = sb("first", [TOK, 2], at=room)
            chosen = sb("chosen", [TOK, 2, 2, EXPERTS], BF16, room)
            tanh_top = sb("tanh_top", [TOK, 2, 2], at=room)
            route_w = sb("route_w", [TOK, 2], at=room)
            place_e = sb("place_e", [TOK, 2, EXPERTS], at=room)
            place_f = sb("place_f", [TOK, 4, 2], at=room)
            place = sb("place", [TOK, 4, 2], I32, room)

        with ExitStack() as room:
            xs = sb("xs", [P, 4, D], at=room)
            xsT_hi, xsT_lo = parts("xsT", [P, 4, KC, P], room)
            silu_g = sb("silu_g", [P, 2, INNER], at=room)
            act_u = sb("act_u", [P, 2, INNER], at=room)
            actT_hi, actT_lo = parts("actT", [P, 2, P], room)
            result = sb("result", [P, 4, D], at=room)
            result_id = sb("result_id", [P, 4], I32, room)
            affine = sb("affine", [P, 4, 2], at=room)

        staging = rows_all[:, TILES // 2:, :].rearrange("p t w -> p (t w)")
        X_UNIT = (FC // 2) * OCT * PATCHES
        sizes = [4 * X_UNIT, FC * D, KC * 2 * D, KC * D, KC * D]
        starts = [sum(sizes[:n]) for n in range(len(sizes) + 1)]
        assert starts[-1] <= staging.shape[1]
        x_in, w_tok_raw, wkv_raw, wq_raw, wo_raw = (staging[:, a:b] for a, b in zip(starts, starts[1:]))
        GU, DOWN = KC * 2 * INNER, D
        expert_raw = rows_all[:, 0:TILES // 2, :].rearrange("p t w -> p (t w)")[:, 0:EXPERTS * (GU + DOWN)]
        RAW_PAIRS = -(-EXPERTS * (GU + DOWN) // (2 * ROW))

        b_tok = ps("b_tok", [P, 512])
        b_turn = ps("b_turn", [P, 512])
        b_qo = ps("b_qo", [P, 512])
        b_kvp = ps("b_kvp", [P, 2, 512])
        b_att = ps("b_att", [P, 2, 512])
        b_gate = ps("b_gate", [P, 512])
        b_x, b_gu = (b_tok[:, :], b_turn[:, :]), (b_kvp[:, 0, :], b_kvp[:, 1, :])
        b_a, b_y = (b_qo[:, :], b_gate[:, :]), (b_att[:, 0, :], b_att[:, 1, :])

        def is_last(p):
            return p.fixed and p.n == PAIRS - 1

        def attention_bank(p):
            return b_kvp[:, 1, :] if is_last(p) else b_gate[:, :]

        region_ends, region_end = b_kvp[0:1, 0, 0:EXPERTS], b_kvp[0:EXPERTS, 1, 0:1]
        tile_ends = b_att[0:1, 0, 0:2 * EXPERTS]

        def b_tile(banks, t, width, start=0):
            return banks[t.slot(2)][:, start:start + width]

        s_const = sem("s_const")
        s_tokw = sem("s_tokw")
        s_tokw2 = sem("s_tokw2")
        s_small = sem("s_small")
        s_weights = sem("s_weights")
        s_expert_w = sem("s_expert_w")
        s_bias_dma = sem("s_bias_dma")
        s_prep = sem("s_prep")
        s_posb = sem("s_posb")
        s_bias_chain = sem("s_bias_chain")
        w_hi = sem("w_hi")
        w_lo = sem("w_lo")
        weight_step = sem("weight_step")
        x_loaded = [sem(f"x_loaded{k}") for k in range(4)]
        x_hi_ready = sem("x_hi_ready")
        x_lo_ready = sem("x_lo_ready")
        unit_done = sem("unit_done")
        patches_ready = sem("patches_ready")
        s_in = [sem(f"s_in{k}") for k in range(2)]
        tokT_ready = sem("tokT_ready")
        back_done = sem("back_done")
        h_ready = sem("h_ready")
        stats1_done = sem("stats1_done")
        mv1_ready = sem("mv1_ready")
        rstd1_step = sem("rstd1_step")
        xn_ready = sem("xn_ready")
        turn_done = sem("turn_done")
        xnT_hi_ready = sem("xnT_hi_ready")
        xnT_lo_ready = sem("xnT_lo_ready")
        q_done = sem("q_done")
        q_parts = sem("q_parts")
        q_ready = sem("q_ready")
        kvp_done = sem("kvp_done")
        kv_parts = sem("kv_parts")
        k_in_ready = sem("k_in_ready")
        k_in_used = sem("k_in_used")
        gu_hi_ready = sem("gu_hi_ready")
        gu_lo_ready = sem("gu_lo_ready")
        k_neg_ready = sem("k_neg_ready")
        k_ready = sem("k_ready")
        v_ready = sem("v_ready")
        room_ready = sem("room_ready")
        affine_ready = sem("affine_ready")
        kvm_done = sem("kvm_done")
        kv_ready = sem("kv_ready")
        apply_done = sem("apply_done")
        den_done = sem("den_done")
        z_done = sem("z_done")
        attn_ready = sem("attn_ready")
        turn_attn_done = sem("turn_attn_done")
        attnT_hi_ready = sem("attnT_hi_ready")
        attnT_lo_ready = sem("attnT_lo_ready")
        wo_done = sem("wo_done")
        h2_ready = sem("h2_ready")
        stats2_done = sem("stats2_done")
        mv2_ready = sem("mv2_ready")
        rstd2_step = sem("rstd2_step")
        xn2_ready = sem("xn2_ready")
        turn2_done = sem("turn2_done")
        xn2T_ready = sem("xn2T_ready")
        gate_done = sem("gate_done")
        top_ready = sem("top_ready")
        ranked_ready = sem("ranked_ready")
        first_ready = sem("first_ready")
        chosen_ready = sem("chosen_ready")
        so_far_ready = sem("so_far_ready")
        tanh_ready = sem("tanh_ready")
        rank_done = sem("rank_done")
        place_ready = sem("place_ready")
        field_step = sem("field_step")
        scattered = [sem(f"scattered{k}") for k in range(4)]
        down_hi_ready = sem("down_hi_ready")
        down_lo_ready = sem("down_lo_ready")
        table_pe = sem("table_pe")
        table_step = sem("table_step")
        table_ready = sem("table_ready")
        tail_zeroed = sem("tail_zeroed")
        row_loaded = [sem(f"row_loaded{k}") for k in range(4)]
        xs_ready = sem("xs_ready")
        turn_x_done = sem("turn_x_done")
        xsT_hi_ready = sem("xsT_hi_ready")
        xsT_lo_ready = sem("xsT_lo_ready")
        gu_done = sem("gu_done")
        silu_ready = sem("silu_ready")
        act_ready = sem("act_ready")
        turn_a_done = sem("turn_a_done")
        actT_hi_ready = sem("actT_hi_ready")
        actT_lo_ready = sem("actT_lo_ready")
        down_done = sem("down_done")
        result_ready = sem("result_ready")
        id_copied = sem("id_copied")
        stored = [sem(f"stored{k}") for k in range(4)]

        SMALL_DMAS, WEIGHT_DMAS = 5, 5
        CONST_DMAS = 2
        UNITS = 2 * IMAGES // OCT
        STEADY_A, STEADY_B, UNROLL_B = (2, 6), (1, 7), 8
        BEFORE_A, AFTER_A = range(0, 4 * STEADY_A[0]), range(4 * STEADY_A[1], PAIRS + 5)
        BEFORE_B, AFTER_B = range(-5, UNROLL_B * STEADY_B[0]), range(UNROLL_B * STEADY_B[1], TILES + 3)
        GU_STEP, DOWN_STEP = PAIRS - EXPERTS, PAIRS - EXPERTS // 2

        def ahead(eng, value):
            return value if isinstance(value, int) else eng.to_reg(value)

        def walk(eng, before, steady, after, step, unroll=4):
            for i in before:
                step(Turn(0, i, unroll))
            with eng.Fori(steady[0], steady[1]) as m:
                for c in range(unroll):
                    step(Turn(m, c, unroll))
            for i in after:
                step(Turn(0, i, unroll))

        def zero_tails(eng, experts):
            eng.wait_ge(table_ready, 1)
            tail = [eng.alloc_register(f"tail{e}") for e in experts]
            eng.reg_load(tail, tail_at[0:1, experts[0]:experts[-1] + 1])
            for register in tail:
                at = eng.snap(register, min_val=0, max_val=EXPERTS * REGION - P)
                eng.dma_start(scratch[bass.ds(at, P), :], tail_rows[:]).then_inc(tail_zeroed, 16)

        def units(eng, unit, order):
            for what in order:
                if what == "steady":
                    with eng.Fori(1, UNITS // 4 - 1) as m:
                        for c in range(4):
                            unit(Turn(m, c))
                elif isinstance(what, int):
                    unit(Turn(0, what))
                else:
                    what()

        block = ctx.enter_context(nc.Block())

        @block.sync
        def _(sp):
            def load_unit(u):
                k = u.slot(4)
                if u.had(4):
                    sp.wait_ge(x_lo_ready, u.upto(4))
                sp.dma_start(x_in[:, k * X_UNIT:(k + 1) * X_UNIT], x[bass.ds(u.n, 1)]).then_inc(x_loaded[k], 16)

            def load_text(p):
                if p.had(2):
                    sp.wait_ge(mv1_ready, p.upto(2))
                sp.dma_start(rows_all[CLS_AT + 1:TOK, bass.ds(2 * p.n, 2), 0:D],
                             txt[:, bass.ds(2 * p.n, 2)]).then_inc(s_in[p.slot(2)], 16)

            W_HALF = FC // 2 * D
            sp.dma_start(w_tok_raw[:, 0:W_HALF], w_tok[:, 0:W_HALF]).then_inc(s_tokw, 16)
            load_unit(Turn(0, 0))
            sp.dma_start(w_tok_raw[:, W_HALF:], w_tok[:, W_HALF:]).then_inc(s_tokw2, 16)
            load_unit(Turn(0, 1))
            for to, what in ((pos_s, pos), (tokb_s, tok_b), (cls_s, cls), (bq_s, bq), (gate_s, gate)):
                sp.dma_start(to[:], what).then_inc(s_small, 16)
            for n in (2, 3):
                load_unit(Turn(0, n))
            sp.dma_start(con_s[:], consts).then_inc(s_const, 16)
            sp.dma_start(ids_s[:], ids).then_inc(s_const, 16)
            load_unit(Turn(0, 4))
            sp.dma_start(wkv_raw, wkv).then_inc(s_weights, 16)
            load_unit(Turn(0, 5))
            sp.dma_start(wq_raw, wq).then_inc(s_weights, 16)
            sp.dma_start(wo_raw, wo).then_inc(s_weights, 16)
            sp.dma_start(bkv_s[:], bkv.to_broadcast([TOK, 2 * D])).then_inc(s_weights, 16)
            sp.dma_start(bias_row[:], bo).then_inc(s_weights, 16)
            load_unit(Turn(0, 6))
            for n in (0, 1):
                load_text(Turn(0, n))
            load_unit(Turn(0, 7))
            with sp.Fori(2, UNITS // 4) as m:
                for c in range(4):
                    load_unit(Turn(m, c))
            for n in (2, 3):
                load_text(Turn(0, n))
            BEFORE_EXPERTS = GU_STEP // 4 - 1
            with sp.Fori(1, BEFORE_EXPERTS) as m:
                for c in range(4):
                    load_text(Turn(m, c))
            sp.wait_ge(h2_ready, RAW_PAIRS)
            for e in range(EXPERTS):
                at = e * (GU + DOWN)
                sp.dma_start(expert_raw[:, at:at + GU], wgu[:, e * GU:(e + 1) * GU]).then_inc(s_expert_w, 16)
                sp.dma_start(expert_raw[:, at + GU:at + GU + DOWN], wdown[:, e * DOWN:(e + 1) * DOWN]).then_inc(s_expert_w, 16)
            with sp.Fori(BEFORE_EXPERTS, PAIRS // 4) as m:
                for c in range(4):
                    load_text(Turn(m, c))

            sp.wait_ge(s_prep, 1)
            sp.dma_start(scratch[EXPERTS * REGION:EXPERTS * REGION + P, :], tail_rows[:]).then_inc(tail_zeroed, 16)
            zero_tails(sp, range(EXPERTS // 2))
            sp.wait_ge(table_ready, 2)
            start = [sp.alloc_register(f"start{k}") for k in range(4)]
            sp.reg_load(start, slot_row[0:1, 0:4])
            sp.wait_ge(tail_zeroed, 16 * (EXPERTS + 1))
            for k in range(4):
                sp.wait_ge(scattered[k], 2 * 16 * PAIRS // 4)
            sp.wait_ge(h2_ready, PAIRS)
            sp.wait_ge(gu_lo_ready, EXPERTS)
            sp.wait_ge(down_lo_ready, EXPERTS)

            def load_tile(t, again):
                k = t.slot(4)
                if again:
                    sp.wait_ge(row_loaded[k], 16 * t.rounds(4, 4))
                at = sp.snap(start[k], min_val=0, max_val=EXPERTS * REGION)
                sp.dma_start(rows_all[:, bass.ds(t.n, 1), :], scratch[bass.ds(at, P), :]).then_inc(row_loaded[k], 16)

            for n in range(4):
                load_tile(Turn(0, n), False)
            with sp.Fori(1, TILES // 4) as m:
                sp.reg_load(start, slot_row[0:1, bass.ds(4 * m, 4)])
                for c in range(4):
                    load_tile(Turn(m, c), True)
            for k in range(4):
                sp.wait_ge(stored[k], 16 * TILES // 4)

        @block.gpsimd
        def _(pool):
            G = nc.gpsimd

            def rstd(mv, ve, to, shift, ready, chain, p, ring):
                k = p.slot(ring)
                until, until2 = ahead(pool, p.upto()), ahead(pool, p.upto(1, 4))
                pool.wait_ge(s_prep, 1)
                pool.wait_ge(ready, until)
                if p.had(1):
                    pool.wait_ge(chain, until2)
                G.tensor_scalar(ve[:, 0, :], mv[:, k, :, 1], LN_EPS, None, ALU.add).then_inc(chain, 1)
                G.tensor_scalar(ve[:, 1, :], mv[:, k, :, 0], -1.0, None, ALU.mult).then_inc(chain, 1)
                pool.wait_ge(chain, p.upto(1, 4) + 2)
                G.tensor_tensor(to[:, k, :], ve[:, 0, :], half_neg[0:TOK, :], ALU.pow).then_inc(chain, 1)
                pool.wait_ge(chain, p.upto(1, 4) + 3)
                G.tensor_tensor(shift[:, k, :], ve[:, 1, :], to[:, k, :], ALU.mult).then_inc(chain, 1)

            def scatter(p):
                k = p.slot(4)
                until = ahead(pool, p.upto())
                pool.wait_ge(s_prep, 1)
                pool.wait_ge(tanh_ready, until)
                G.tensor_scalar(route_w[:], tanh_top[:, p.slot(2), :], 1.0, 0.5, ALU.add, ALU.mult).then_inc(field_step, 1)
                G.tensor_copy(rows[:, k, :, ID].bitcast(I32), ids_s[:, bass.ds(2 * p.n, 2)]).then_inc(field_step, 1)
                pool.wait_ge(field_step, p.upto(1, 5) + 1)
                G.tensor_tensor(rows[:, k, :, GAIN], route_w[:], rstd2[:, k, :], ALU.mult).then_inc(field_step, 1)
                G.tensor_tensor(rows[:, k, :, SHIFT], route_w[:], shift2[:, k, :], ALU.mult).then_inc(field_step, 1)
                until = ahead(pool, p.upto())
                pool.wait_ge(s_prep, 1)
                pool.wait_ge(place_ready, until)
                G.tensor_copy(place[:, k, :], place_f[:, k, :]).then_inc(field_step, 1)
                until = ahead(pool, p.upto(0, 5))
                pool.wait_ge(s_prep, 1)
                pool.wait_ge(field_step, until)
                for b in range(2):
                    G.indirect_dma_start(
                        out=scratch[0:EXPERTS * REGION, :],
                        out_offset=bass.IndirectOffsetOnAxis(ap=place[:, k, b:b + 1], axis=0),
                        in_=rows[:, k, b, :], in_offset=None).then_inc(scattered[k], 16)

            def step(i):
                if (i - 4).within(PAIRS):
                    p = i - 4
                    pool.wait_ge(chosen_ready, p.upto())
                    if p.had(1):
                        pool.wait_ge(rank_done, p.upto(1))
                    G.tensor_tensor(so_far[0:TOK, (p + 1).slot(2)], so_far[0:TOK, p.slot(2)], chosen[:, p.slot(2)],
                                    ALU.add).then_inc(so_far_ready, 1)
                if (i + 3).within(PAIRS):
                    p = i + 3
                    until = ahead(pool, p.upto(1))
                    pool.wait_ge(s_prep, 1)
                    if p.had(1):
                        pool.wait_ge(back_done, until)
                    G.tensor_copy(tokT[:, :, :, 0:PATCHES], tokT_all[:, :, bass.ds(2 * p.n, 2), :]).then_inc(tokT_ready, 1)
                if (i + 2).within(PAIRS):
                    rstd(mv1, ve1, rstd1, shift1, mv1_ready, rstd1_step, i + 2, 2)
                if i.within(PAIRS):
                    p = i
                    until, until2 = ahead(pool, p.upto()), ahead(pool, p.upto(1))
                    pool.wait_ge(s_prep, 1)
                    pool.wait_ge(kv_parts, until)
                    if p.had(1):
                        pool.wait_ge(kvm_done, until2)
                    G.tensor_tensor(k_sb[:], k_exp[:], k_relu[:], ALU.add).then_inc(k_ready, 1)
                first_scatter = i.fixed and i.n == PAIRS
                if first_scatter:
                    scatter(i - 4)
                if (i - 2).within(PAIRS):
                    rstd(mv2, ve2, rstd2, shift2, mv2_ready, rstd2_step, i - 2, 4)
                if (i - 4).within(PAIRS) and not first_scatter:
                    scatter(i - 4)
                if i.fixed and GU_STEP <= i.n < PAIRS:
                    e = i.n - GU_STEP
                    at = e * (GU + DOWN)
                    pool.wait_ge(gu_hi_ready, e + 1)
                    G.tensor_tensor(wgu_lo[:, e].rearrange("p k d -> p (k d)"), expert_raw[:, at:at + GU],
                                    wgu_hi[:, e].rearrange("p k d -> p (k d)").bitcast(F32), ALU.subtract).then_inc(gu_lo_ready, 1)

            pool.wait_ge(s_prep, 1)
            pool.wait_ge(patches_ready, 1)
            step(Turn(0, -3))
            pool.wait_ge(s_weights, 16 * WEIGHT_DMAS)
            left = bias_row
            for r in range(3):
                G.tensor_copy(bias_part[:, r, :], left[:]).then_inc(s_bias_chain, 1)
                if r < 2:
                    pool.wait_ge(s_bias_chain, 2 * r + 1)
                    G.tensor_tensor(bias_left[:], left[:], bias_part[:, r, :], ALU.subtract).then_inc(s_bias_chain, 1)
                    pool.wait_ge(s_bias_chain, 2 * r + 2)
                left = bias_left
            for n, (lo, raw, hi) in enumerate(((wkv_lo, wkv_raw, wkv_hi), (wq_lo, wq_raw, wq_hi), (wo_lo, wo_raw, wo_hi))):
                G.tensor_copy(hi[:].rearrange("p k d -> p (k d)"), raw).then_inc(weight_step, 1)
                pool.wait_ge(weight_step, 2 * n + 1)
                G.tensor_tensor(lo[:].rearrange("p k d -> p (k d)"), raw, hi[:].rearrange("p k d -> p (k d)").bitcast(F32),
                                ALU.subtract).then_inc(weight_step, 1)
            step(Turn(0, -2))
            step(Turn(0, -1))
            pool.wait_ge(s_const, 16 * CONST_DMAS)
            pool.wait_ge(s_posb, 2)
            pool.wait_ge(patches_ready, IMAGES // OCT)
            walk(pool, BEFORE_A, STEADY_A, AFTER_A, step)

            def tile_step(j):
                if (j - 1).within(TILES):
                    t = j - 1
                    until, until2 = ahead(pool, 16 * t.rounds(4)), ahead(pool, 16 * t.rounds(4, 4))
                    pool.wait_ge(s_prep, 1)
                    pool.wait_ge(row_loaded[t.slot(4)], until)
                    if t.had(4):
                        pool.wait_ge(stored[t.slot(4)], until2)
                    G.tensor_copy(result_id[:, t.slot(4):t.slot(4) + 1],
                                  rows_all[:, bass.ds(t.n, 1), ID].bitcast(I32)).then_inc(id_copied, 1)
                if (j - 2).within(TILES):
                    t = j - 2
                    k = t.slot(4)
                    until = ahead(pool, t.upto())
                    pool.wait_ge(s_prep, 1)
                    pool.wait_ge(id_copied, until)
                    pool.wait_ge(result_ready, until)
                    G.indirect_dma_start(
                        out=out, out_offset=bass.IndirectOffsetOnAxis(ap=result_id[:, k:k + 1], axis=0),
                        in_=result[:, k, :], in_offset=None,
                        bounds_check=TOKENS - 1, oob_is_err=False).then_inc(stored[k], 16)

            walk(pool, BEFORE_B, STEADY_B, AFTER_B, tile_step, UNROLL_B)

        @block.scalar
        def _(act):
            S = nc.scalar
            def unit(u):
                k = u.slot(4)
                act.wait_ge(x_loaded[k], 16 * u.rounds(4))
                if u.had(2):
                    act.wait_ge(unit_done, u.upto(2))
                S.copy(xp_hi[:, u.slot(2)].rearrange("p f n -> p (f n)"), x_in[:, k * X_UNIT:(k + 1) * X_UNIT]).then_inc(x_hi_ready, 1)

            def turned(bank):
                return bank[:, 0:4 * TOK].rearrange("p (k t) -> p k t", k=KC)

            def down_high(n):
                act.wait_ge(back_done, PAIRS)
                for e in (2 * n - 2, 2 * n - 1):
                    at = e * (GU + DOWN) + GU
                    last = S.copy(wdown_hi[:, e], expert_raw[:, at:at + DOWN])
                last.then_inc(down_hi_ready, 2)

            def attention_high(p):
                act.wait_ge(turn_attn_done, p.upto())
                if p.had(1):
                    act.wait_ge(wo_done, p.upto(1))
                S.copy(attnT_hi[:], turned(attention_bank(p))).then_inc(attnT_hi_ready, 1)

            def step(i):
                if (i - 4).within(PAIRS):
                    p = i - 4
                    act.wait_ge(top_ready, p.upto())
                    if p.had(2):
                        act.wait_ge(field_step, p.upto(2, 5))
                    S.activation(tanh_top[:, p.slot(2), :], top[:, p.slot(2), :], ACT.Tanh, scale=0.5).then_inc(tanh_ready, 1)
                if (i + 1).within(PAIRS):
                    p = i + 1
                    act.wait_ge(turn_done, p.upto())
                    if p.had(2):
                        act.wait_ge(q_done, p.upto(2))
                    S.copy(xnT_hi[:, p.slot(2), :, 0:2 * TOK], turned(b_turn)).then_inc(xnT_hi_ready, 1)
                if (i - 2).within(PAIRS) and not (i.fixed and i.n == PAIRS + 1):
                    attention_high(i - 2)
                if (i - 3).within(PAIRS):
                    p = i - 3
                    k = p.slot(4)
                    act.wait_ge(rstd2_step, p.upto(0, 4))
                    if p.had(1):
                        act.wait_ge(turn2_done, p.upto(1))
                    for b in range(2):
                        last = S.activation(xn2[:, b, :], rows[:, k, b, 0:D], ACT.Identity,
                                            bias=shift2[:, k, b:b + 1], scale=rstd2[:, k, b:b + 1])
                    last.then_inc(xn2_ready, 1)
                if i.fixed and GU_STEP <= i.n < PAIRS:
                    e = i.n - GU_STEP
                    act.wait_ge(s_expert_w, 32 * EXPERTS)
                    at = e * (GU + DOWN)
                    S.copy(wgu_hi[:, e].rearrange("p k d -> p (k d)"), expert_raw[:, at:at + GU]).then_inc(gu_hi_ready, 1)
                if i.fixed and DOWN_STEP < i.n < PAIRS:
                    down_high(i.n - DOWN_STEP)
                if i.fixed and i.n == PAIRS:
                    attention_high(i - 1)
                if i.within(PAIRS):
                    p = i
                    act.wait_ge(k_in_ready, p.upto())
                    if p.had(1):
                        act.wait_ge(k_ready, p.upto(1))
                    S.activation(k_neg[:], k_in[:], ACT.Relu, scale=-1.0).then_inc(k_neg_ready, 1)
                    S.activation(k_relu[:], k_in[:], ACT.Relu).then_inc(k_in_used, 1)
                    act.wait_ge(k_neg_ready, p.upto())
                    S.activation(k_exp[:], k_neg[:], ACT.Exp, scale=-1.0).then_inc(kv_parts, 1)
                if (i + 2).within(PAIRS):
                    p = i + 2
                    until, until2 = ahead(act, p.upto(0, 4)), ahead(act, p.upto(1))
                    act.wait_ge(s_small, 16)
                    act.wait_ge(rstd1_step, until)
                    if p.had(1):
                        act.wait_ge(turn_done, until2)
                    for b in range(2):
                        last = S.activation(xn[:, b, :], rows_all[0:TOK, bass.ds(2 * p.n + b, 1), 0:D], ACT.Identity,
                                            bias=shift1[:, p.slot(2), b:b + 1], scale=rstd1[:, p.slot(2), b:b + 1])
                    last.then_inc(xn_ready, 1)
                if (i - 3).within(PAIRS):
                    p = i - 3
                    act.wait_ge(turn2_done, p.upto())
                    if p.had(1):
                        act.wait_ge(gate_done, p.upto(1))
                    S.copy(xn2T[:], turned(b_turn)).then_inc(xn2T_ready, 1)
                if i.fixed and i.n == PAIRS:
                    down_high(i.n - DOWN_STEP)
                if i.within(PAIRS):
                    p = i
                    act.wait_ge(q_done, p.upto())
                    if p.had(1):
                        act.wait_ge(q_ready, p.upto(1))
                    for c in range(KC):
                        at = b_qo[:, c * QW:c * QW + 2 * TOK]
                        S.activation(q_exp[:, c, :], at, ACT.Exp, bias=bq_s[:, c:c + 1])
                        last = S.activation(q_relu[:, c, :], at, ACT.Relu, bias=bq_s[:, c:c + 1])
                    last.then_inc(q_parts, 1)
                if (i + 3).within(PAIRS):
                    p = i + 3
                    until = ahead(act, p.upto())
                    act.wait_ge(s_small, 16)
                    act.wait_ge(back_done, until)
                    S.activation(rows_all[0:PATCHES + 1, bass.ds(2 * p.n, 2), 0:D],
                                 b_tok[0:PATCHES + 1, :].rearrange("p (b d) -> p b d", b=2), ACT.Copy).then_inc(h_ready, 1)

            def w_tok_part(h, arrived):
                half, at = slice(h * FC // 2, (h + 1) * FC // 2), slice(h * FC // 2 * D, (h + 1) * FC // 2 * D)
                act.wait_ge(arrived, 16)
                S.copy(w_tok_hi[:, half].rearrange("p f d -> p (f d)"), w_tok_raw[:, at]).then_inc(w_hi, 1)

            def bias_rows():
                act.wait_ge(s_bias_chain, 5)
                for r in range(3):
                    act.dma_start(bias3[r:r + 1, :], bias_part[:, r, :]).then_inc(s_bias_dma, 16)
                act.wait_ge(s_small, 16 * SMALL_DMAS)

            units(act, unit, [
                lambda: w_tok_part(0, s_tokw), 0, lambda: w_tok_part(1, s_tokw2), 1,
                2, 3, "steady", lambda: step(Turn(0, -3)), 12, bias_rows, 13,
                14, lambda: step(Turn(0, -2)), 15, lambda: step(Turn(0, -1))])
            walk(act, BEFORE_A, STEADY_A, AFTER_A, step)
            zero_tails(act, range(EXPERTS // 2, EXPERTS))
            S.activation(silu_ahead[:], bq_s[:, 0:1], ACT.Silu)

            def tile_step(j):
                if j.within(TILES):
                    t = j
                    act.wait_ge(gu_done, t.upto())
                    S.activation(silu_g[:, t.slot(2)], b_tile(b_gu, t, INNER), ACT.Silu).then_inc(silu_ready, 1)
                if (j + 2).within(TILES):
                    t = j + 2
                    act.wait_ge(turn_x_done, t.upto())
                    S.copy(xsT_hi[:, t.slot(4)], b_tile(b_x, t, KC * P).rearrange("p (k t) -> p k t", k=KC)).then_inc(xsT_hi_ready, 1)
                if (j - 1).within(TILES):
                    t = j - 1
                    act.wait_ge(turn_a_done, t.upto())
                    if t.had(2):
                        act.wait_ge(down_done, t.upto(2))
                    S.copy(actT_hi[:, t.slot(2)], b_tile(b_a, t, P)).then_inc(actT_hi_ready, 1)
                if (j + 4).within(TILES):
                    t = j + 4
                    until = ahead(act, t.upto())
                    act.wait_ge(s_small, 16)
                    act.wait_ge(affine_ready, until)
                    S.activation(xs[:, t.slot(4)], rows_all[:, bass.ds(t.n, 1), 0:D], ACT.Identity,
                                 bias=affine[:, t.slot(4), 0:1], scale=affine[:, t.slot(4), 1:2]).then_inc(xs_ready, 1)

            walk(act, BEFORE_B, STEADY_B, AFTER_B, tile_step, UNROLL_B)

        @block.vector
        def _(dve):
            V = nc.vector

            def low(to, whole, high):
                return V.tensor_tensor(to, whole, high.bitcast(F32), ALU.subtract)

            V.memset(tail_rows[:, 0:ID], 0.0)
            V.memset(tail_rows[:, ID:].bitcast(I32), NO_TOKEN)
            V.memset(half_neg[:], -0.5)
            V.memset(ones_bf[:], 1.0)
            V.memset(bias3[:], 0.0).then_inc(s_prep, 1)

            def w_tok_part(h):
                half, at = slice(h * FC // 2, (h + 1) * FC // 2), slice(h * FC // 2 * D, (h + 1) * FC // 2 * D)
                dve.wait_ge(w_hi, h + 1)
                low(w_tok_lo[:, half].rearrange("p f d -> p (f d)"), w_tok_raw[:, at],
                    w_tok_hi[:, half].rearrange("p f d -> p (f d)")).then_inc(w_lo, 1)

            def position():
                dve.wait_ge(s_small, 16 * SMALL_DMAS)
                for c in range(KC):
                    last = V.tensor_scalar(posb[:, c, :], pos_s[:, c, 1:], tokb_s[:, c:c + 1], None, ALU.add)
                    for b in range(2):
                        V.tensor_tensor(tokT[:, c, b, PATCHES:], pos_s[:, c, 0:1], cls_s[:, c:c + 1], ALU.add)
                for k in range(2):
                    V.memset(xnT_hi[:, k, :, 2 * TOK:].bitcast(F32), 0.0)
                    last = V.memset(xnT_lo[:, k, :, 2 * TOK:].bitcast(F32), 0.0)
                last.then_inc(s_posb, 1)
                dve.wait_ge(s_posb, 1)

            def tables():
                dve.wait_ge(s_const, 16 * CONST_DMAS)
                V.tensor_copy(earlier[:], con["c_earlier"])
                for k in range(2):
                    last = V.tensor_copy(so_far[:, k], con["c_region"].rearrange("p (b e) -> p b e", b=2))
                last.then_inc(s_posb, 1)

            def patches_out(q, k):
                dve.wait_ge(unit_done, 2 * q + 2)
                for c, bank in enumerate((b_kvp, b_att)):
                    last = V.tensor_tensor(
                        tokT_all[:, c, bass.ds(OCT * q, OCT), :],
                        bank[:, k, 0:OCT * PATCHES].rearrange("p (b n) -> p b n", b=OCT),
                        posb[:, c:c + 1, :].to_broadcast([P, OCT, PATCHES]), ALU.add)
                last.then_inc(patches_ready, 1)

            def unit(u):
                k = u.slot(4)
                dve.wait_ge(x_hi_ready, u.upto())
                low(xp_lo[:, u.slot(2)].rearrange("p f n -> p (f n)"), x_in[:, k * X_UNIT:(k + 1) * X_UNIT],
                    xp_hi[:, u.slot(2)].rearrange("p f n -> p (f n)")).then_inc(x_lo_ready, 1)
                if u.c % 2 == 0 and u.had(2):
                    patches_out(2 * u.m + u.c // 2 - 1, (u.c // 2 - 1) % 2)

            def stats(src, to, mv, done, ready, p):
                for b in range(2):
                    last = V.bn_stats(to[:, b, :], src(b))
                last.then_inc(done, 1)
                until = ahead(dve, p.upto())
                dve.wait_ge(s_posb, 2)
                dve.wait_ge(done, until)
                for b in range(2):
                    last = V.bn_aggr(mv[:, b, :], to[:, b, :])
                last.then_inc(ready, 1)

            def turned(bank):
                return bank[:, 0:4 * TOK].rearrange("p (k t) -> p k t", k=KC)

            def tokens_low(p):
                dve.wait_ge(xnT_hi_ready, p.upto())
                low(xnT_lo[:, p.slot(2), :, 0:2 * TOK], turned(b_turn), xnT_hi[:, p.slot(2), :, 0:2 * TOK]).then_inc(xnT_lo_ready, 1)

            def stats_1(p):
                until, until2, until3 = ahead(dve, p.upto()), ahead(dve, 16 * p.rounds(2)), ahead(dve, p.upto(2))
                dve.wait_ge(s_posb, 2)
                dve.wait_ge(h_ready, until)
                dve.wait_ge(s_in[p.slot(2)], until2)
                if p.had(2):
                    dve.wait_ge(xn_ready, until3)
                stats(lambda b: rows_all[0:TOK, bass.ds(2 * p.n + b, 1), 0:D], stats1, mv1[:, p.slot(2)],
                      stats1_done, mv1_ready, p)

            def attention_low(p):
                dve.wait_ge(attnT_hi_ready, p.upto())
                low(attnT_lo[:], turned(attention_bank(p)), attnT_hi[:]).then_inc(attnT_lo_ready, 1)

            def residual(p):
                k = p.slot(4)
                dve.wait_ge(wo_done, p.upto())
                if p.had(4):
                    dve.wait_ge(scattered[k], 32 * p.rounds(4, 4))
                V.tensor_tensor(rows[:, k, :, 0:D], b_qo[0:TOK, 0:2 * D].rearrange("p (b d) -> p b d", b=2),
                                rows_all[0:TOK, bass.ds(2 * p.n, 2), 0:D], ALU.add).then_inc(h2_ready, 1)

            def stats_2(p):
                k = p.slot(4)
                until = ahead(dve, p.upto())
                dve.wait_ge(s_posb, 2)
                dve.wait_ge(h2_ready, until)
                stats(lambda b: rows[:, k, b, 0:D], stats2, mv2[:, k], stats2_done, mv2_ready, p)

            def attention(p):
                dve.wait_ge(apply_done, p.upto())
                heads = b_att[0:TOK, :, 0:KC * KVW].rearrange("p b (k w) -> p b k w", k=KC)
                V.tensor_scalar(den[:].rearrange("p b (k h) -> p b k h", k=KC), heads[:, :, :, P:KVW],
                                Z_EPS, None, ALU.add).then_inc(den_done, 1)
                dve.wait_ge(den_done, p.upto())
                V.reciprocal(z[:], den[:]).then_inc(z_done, 1)
                dve.wait_ge(z_done, p.upto())
                if p.had(1):
                    dve.wait_ge(turn_attn_done, p.upto(1))
                for b in range(2):
                    last = V.tensor_tensor(
                        attn[:, b, :].rearrange("p (k h e) -> p k h e", k=KC, h=HPC),
                        heads[:, b, :, 0:P].rearrange("p k (h e) -> p k h e", h=HPC),
                        z[:, b, :].rearrange("p (k h a) -> p k h a", k=KC, a=1).to_broadcast([TOK, KC, HPC, DH]),
                        ALU.mult)
                last.then_inc(attn_ready, 1)

            def places(p):
                dve.wait_ge(rank_done, p.upto())
                for b in range(2):
                    last = V.tensor_tensor_reduce(place_e[:, b, :], b_tok[0:TOK, b * EXPERTS:(b + 1) * EXPERTS],
                                                  chosen[:, p.slot(2), b, :], 1.0, 0.0, ALU.mult, ALU.add,
                                                  place_f[:, p.slot(4), b:b + 1])
                last.then_inc(place_ready, 1)

            def step(i):
                starting = i.fixed and i.n < 0
                if (i - 4).within(PAIRS):
                    p = i - 4
                    dve.wait_ge(gate_done, p.upto())
                    if p.had(2):
                        dve.wait_ge(tanh_ready, p.upto(2))
                    logits = b_gate[0:TOK, 0:2 * EXPERTS].rearrange("p (b e) -> p b e", b=2)
                    V.tensor_reduce(top[:, p.slot(2), :], logits, AX_X, ALU.max).then_inc(top_ready, 1)
                    dve.wait_ge(top_ready, p.upto())
                    for b in range(2):
                        last = V.scalar_tensor_tensor(ranked[:, b, :], logits[:, b, :], top[:, p.slot(2), b:b + 1],
                                                      con["c_weight8"], ALU.is_equal, ALU.mult)
                    last.then_inc(ranked_ready, 1)
                if (i - 1).within(PAIRS):
                    p = i - 1
                    dve.wait_ge(q_parts, p.upto())
                    if p.had(1):
                        dve.wait_ge(apply_done, p.upto(1))
                    V.scalar_tensor_tensor(qT[:], q_exp[:], 1.0, q_relu[:], ALU.min, ALU.add).then_inc(q_ready, 1)
                    dve.wait_ge(kvm_done, p.upto())
                    V.tensor_tensor(kv_sb[:].rearrange("p b k w -> p (b k) w"),
                                    b_att[:, :, 0:KC * KVW].rearrange("p b (k w) -> p b k w", k=KC),
                                    mask.rearrange("p (a w) -> p a w", a=1).to_broadcast([P, 2 * KC, KVW]),
                                    ALU.mult).then_inc(kv_ready, 1)
                if (i + 1).within(PAIRS) and not starting:
                    tokens_low(i + 1)
                if (i - 2).within(PAIRS) and not (i.fixed and i.n == PAIRS + 1):
                    attention_low(i - 2)
                if (i - 4).within(PAIRS):
                    p = i - 4
                    dve.wait_ge(ranked_ready, p.upto())
                    V.tensor_reduce(first[:], ranked[:], AX_X, ALU.max).then_inc(first_ready, 1)
                    dve.wait_ge(first_ready, p.upto())
                    if p.had(2):
                        dve.wait_ge(so_far_ready, p.upto(2))
                        dve.wait_ge(rank_done, p.upto(2))
                    V.tensor_tensor(chosen[:, p.slot(2)], ranked[:],
                                    first[:].rearrange("p (b a) -> p b a", a=1).to_broadcast([TOK, 2, EXPERTS]),
                                    ALU.is_equal).then_inc(chosen_ready, 1)
                if (i + 2).within(PAIRS):
                    stats_1(i + 2)
                if (i + 1).within(PAIRS) and starting:
                    tokens_low(i + 1)
                if i.within(PAIRS):
                    p = i
                    dve.wait_ge(kvp_done, p.upto())
                    if p.had(1):
                        dve.wait_ge(k_in_used, p.upto(1))
                    V.tensor_tensor(k_in[:], b_kvp[0:TOK, :, 0:D],
                                    bkv_s[:, 0:D].rearrange("p (b d) -> p b d", b=1).to_broadcast([TOK, 2, D]),
                                    ALU.add).then_inc(k_in_ready, 1)
                    if p.had(1):
                        dve.wait_ge(kvm_done, p.upto(1))
                    for b in range(2):
                        last = V.tensor_tensor(v_sb[:, b, :, 0:P],
                                               b_kvp[0:TOK, b, D:2 * D].rearrange("p (k e) -> p k e", k=KC),
                                               bkv_s[:, D:2 * D].rearrange("p (k e) -> p k e", k=KC), ALU.add)
                    last.then_inc(v_ready, 1)
                draining = i.fixed and i.n >= PAIRS
                if draining and (i - 1).within(PAIRS):
                    attention(i - 1)
                if draining and (i - 4).within(PAIRS):
                    places(i - 4)
                if (i - 2).within(PAIRS):
                    residual(i - 2)
                    if i.fixed and i.n == PAIRS:
                        attention_low(i - 1)
                if not draining and (i - 1).within(PAIRS):
                    attention(i - 1)
                if not draining and (i - 4).within(PAIRS):
                    places(i - 4)
                if (i - 2).within(PAIRS):
                    stats_2(i - 2)
                if i.fixed and DOWN_STEP < i.n <= PAIRS:
                    down_parts(i.n - DOWN_STEP)

            def down_parts(n):
                dve.wait_ge(down_hi_ready, 2 * n)
                for e in (2 * n - 2, 2 * n - 1):
                    at = e * (GU + DOWN) + GU
                    last = low(wdown_lo[:, e], expert_raw[:, at:at + DOWN], wdown_hi[:, e])
                last.then_inc(down_lo_ready, 2)

            def room_setup():
                patches_out(UNITS // 2 - 1, (UNITS // 2 - 1) % 2)
                dve.wait_ge(s_bias_dma, 48)
                V.memset(v_sb[:, :, :, P:], 1.0)
                V.memset(rows[:, :, :, ID + 1:], 0.0).then_inc(room_ready, 1)

            units(dve, unit, [
                lambda: w_tok_part(0), 0, lambda: w_tok_part(1), 1, position, 2, 3, tables, "steady",
                12, lambda: step(Turn(0, -2)), 13, 14, 15, lambda: step(Turn(0, -1)), room_setup])
            walk(dve, BEFORE_A, STEADY_A, AFTER_A, step)

            done = [0]

            def link(ins):
                ins.then_inc(table_step, 1)
                done[0] += 1
                dve.wait_ge(table_step, done[0])

            dve.wait_ge(table_pe, 1)
            V.tensor_copy(tail_at[:], region_ends).then_inc(table_ready, 1)
            link(V.tensor_scalar(held[:], region_end, con["c_regcol"][:, 0:1], float(P - 1), ALU.subtract, ALU.add))
            link(V.tensor_copy(held_i[:], held[:]))
            link(V.tensor_scalar(tiles_i[:], held_i[:], P.bit_length() - 1, None, ALU.logical_shift_right))
            link(V.tensor_copy(tiles_f[:], tiles_i[:]))
            dve.wait_ge(table_pe, 2)
            link(V.tensor_copy(ends[:], tile_ends))

            def over_slots(ap):
                return ap.rearrange("p (a e) -> p a e", a=1).to_broadcast([1, TILES, EXPERTS])

            link(V.tensor_tensor(past[:], con["c_slot"].rearrange("p (t e) -> p t e", t=TILES),
                                 over_slots(ends[:, 0:EXPERTS]), ALU.is_ge))
            link(V.tensor_reduce(slot_e[:], past[:], AX_X, ALU.add))
            link(V.tensor_tensor(past_n[:], past[:], over_slots(ends[:, EXPERTS:]), ALU.mult))
            link(V.tensor_reduce(slot_s[:], past_n[:], AX_X, ALU.add))
            link(V.scalar_tensor_tensor(slot_r[:], slot_s[:], -float(P), con["c_slotrow"], ALU.mult, ALU.add))
            link(V.scalar_tensor_tensor(slot_r2[:], slot_e[:], float(REGION), slot_r[:], ALU.mult, ALU.add))
            V.tensor_scalar(slot_row[:], slot_r2[:], float(EXPERTS * REGION), None, ALU.min).then_inc(table_ready, 1)
            V.tensor_scalar(slot_expert[:], slot_e[:], float(EXPERTS - 1), None, ALU.min).then_inc(table_ready, 1)

            def tile_step(j):
                if j.within(TILES):
                    t = j
                    dve.wait_ge(silu_ready, t.upto())
                    V.tensor_tensor(act_u[:, t.slot(2)], b_tile(b_gu, t, INNER, INNER), silu_g[:, t.slot(2)],
                                    ALU.mult).then_inc(act_ready, 1)
                if (j + 2).within(TILES):
                    t = j + 2
                    dve.wait_ge(xsT_hi_ready, t.upto())
                    low(xsT_lo[:, t.slot(4)], b_tile(b_x, t, KC * P).rearrange("p (k t) -> p k t", k=KC),
                        xsT_hi[:, t.slot(4)]).then_inc(xsT_lo_ready, 1)
                if (j - 1).within(TILES):
                    t = j - 1
                    dve.wait_ge(actT_hi_ready, t.upto())
                    low(actT_lo[:, t.slot(2)], b_tile(b_a, t, P), actT_hi[:, t.slot(2)]).then_inc(actT_lo_ready, 1)
                if (j - 2).within(TILES):
                    t = j - 2
                    dve.wait_ge(down_done, t.upto())
                    if t.had(4):
                        dve.wait_ge(stored[t.slot(4)], 16 * t.rounds(4, 4))
                    V.tensor_tensor(result[:, t.slot(4)], b_tile(b_y, t, D), rows_all[:, bass.ds(t.n, 1), 0:D],
                                    ALU.add).then_inc(result_ready, 1)
                if (j + 5).within(TILES):
                    t = j + 5
                    until = ahead(dve, 16 * t.rounds(4))
                    dve.wait_ge(s_posb, 2)
                    dve.wait_ge(row_loaded[t.slot(4)], until)
                    V.tensor_copy(affine[:, t.slot(4), :], rows_all[:, bass.ds(t.n, 1), SHIFT:GAIN + 1]).then_inc(affine_ready, 1)

            walk(dve, BEFORE_B, STEADY_B, AFTER_B, tile_step, UNROLL_B)

        @block.tensor
        def _(pe):
            T = nc.tensor

            def product(to, left, right, start, stop):
                (left_hi, left_lo), (right_hi, right_lo) = left, right
                T.matmul(to, left_hi, right_hi, start=start, stop=False)
                T.matmul(to, left_hi, right_lo, start=False, stop=False)
                return T.matmul(to, left_lo, right_hi, start=False, stop=stop)

            def unit(u):
                if u.fixed and u.n < 2:
                    pe.wait_ge(w_lo, u.n + 1)
                pe.wait_ge(x_lo_ready, u.upto())
                if u.c % 2 == 0 and u.had(4):
                    pe.wait_ge(patches_ready, 2 * u.m + u.c // 2 - 1)
                for c, bank in enumerate((b_kvp, b_att)):
                    for k in range(FC // 2):
                        f = (u.c % 2) * (FC // 2) + k
                        w, xk = slice(c * P, (c + 1) * P), u.slot(2)
                        last = product(bank[:, (u.c // 2) % 2, 0:OCT * PATCHES], (w_tok_hi[:, f, w], w_tok_lo[:, f, w]),
                                       (xp_hi[:, xk, k, :], xp_lo[:, xk, k, :]), f == 0, f == FC - 1)
                last.then_inc(unit_done, 1)

            def turn_attention(p):
                pe.wait_ge(attn_ready, p.upto())
                if not is_last(p):
                    if p.had(2):
                        pe.wait_ge(ranked_ready, p.upto(2))
                    elif p.had(1):
                        pe.wait_ge(attnT_lo_ready, p.upto(1))
                else:
                    pe.wait_ge(v_ready, PAIRS)
                bank = attention_bank(p)
                for c in range(KC):
                    for b in range(2):
                        at = (2 * c + b) * TOK
                        last = T.transpose(bank[:, at:at + TOK], attn[:, b, c * P:(c + 1) * P], ident[0:TOK, 0:TOK])
                last.then_inc(turn_attn_done, 1)

            def apply(p):
                pe.wait_ge(kv_ready, p.upto())
                pe.wait_ge(q_ready, p.upto())
                for b in range(2):
                    for c in range(KC):
                        last = T.matmul(b_att[0:TOK, b, c * KVW:(c + 1) * KVW], qT[:, c, b * TOK:(b + 1) * TOK],
                                        kv_sb[:, b, c, :], start=True, stop=True)
                last.then_inc(apply_done, 1)

            def step(i):
                if (i - 1).within(PAIRS):
                    p = i - 1
                    pe.wait_ge(k_ready, p.upto())
                    pe.wait_ge(v_ready, p.upto())
                    if not p.had(1):
                        pe.wait_ge(room_ready, 1)
                    if p.had(1):
                        pe.wait_ge(attn_ready, p.upto(1))
                    for b in range(2):
                        for c in range(KC):
                            last = T.matmul(b_att[:, b, c * KVW:(c + 1) * KVW], k_sb[:, b, c * P:(c + 1) * P],
                                            v_sb[:, b, c, :], start=True, stop=True)
                    last.then_inc(kvm_done, 1)
                if (i + 1).within(PAIRS):
                    p = i + 1
                    pe.wait_ge(xn_ready, p.upto())
                    if p.had(5):
                        pe.wait_ge(xn2T_ready, p.upto(5))
                    elif p.had(1):
                        pe.wait_ge(xnT_lo_ready, p.upto(1))
                    for k in range(KC):
                        for b in range(2):
                            at = (2 * k + b) * TOK
                            last = T.transpose(b_turn[:, at:at + TOK], xn[:, b, k * P:(k + 1) * P], ident[0:TOK, 0:TOK])
                    last.then_inc(turn_done, 1)
                if (i - 2).within(PAIRS) and not (i.fixed and i.n == PAIRS + 1):
                    turn_attention(i - 2)
                draining = i.fixed and i.n >= PAIRS
                if draining and (i - 1).within(PAIRS):
                    apply(i - 1)
                if i.within(PAIRS):
                    p = i
                    pe.wait_ge(xnT_lo_ready, p.upto())
                    if p.had(1):
                        pe.wait_ge(v_ready, p.upto(1))
                    for b in range(2):
                        for k in range(KC):
                            at = slice(b * TOK, (b + 1) * TOK)
                            last = product(b_kvp[0:TOK, b, :], (xnT_hi[:, p.slot(2), k, at], xnT_lo[:, p.slot(2), k, at]),
                                           (wkv_hi[:, k, :], wkv_lo[:, k, :]), k == 0, k == KC - 1)
                    last.then_inc(kvp_done, 1)
                if (i - 2).within(PAIRS):
                    p = i - 2
                    pe.wait_ge(attnT_lo_ready, p.upto())
                    if (p + 1).within(PAIRS):
                        pe.wait_ge(q_parts, p.upto(-1))
                    else:
                        pe.wait_ge(h2_ready, p.upto(1))
                    for b in range(2):
                        to = b_qo[0:TOK, b * D:(b + 1) * D]
                        T.matmul(to, ones_bf[:, :], bias3[:, :], start=True, stop=False)
                        for c in range(KC):
                            at = slice(b * TOK, (b + 1) * TOK)
                            last = product(to, (attnT_hi[:, c, at], attnT_lo[:, c, at]), (wo_hi[:, c, :], wo_lo[:, c, :]),
                                           False, c == KC - 1)
                    last.then_inc(wo_done, 1)
                if i.fixed and i.n == PAIRS:
                    turn_attention(i - 1)
                if not draining and (i - 1).within(PAIRS):
                    apply(i - 1)
                if (i - 4).within(PAIRS):
                    p = i - 4
                    pe.wait_ge(chosen_ready, p.upto())
                    if p.had(1):
                        pe.wait_ge(so_far_ready, p.upto(1))
                    if (p + 6).within(PAIRS):
                        pe.wait_ge(h_ready, p.upto(-6))
                    else:
                        pe.wait_ge(place_ready, p.upto(1))
                    ranks, second = b_tok[0:TOK, 0:2 * EXPERTS], b_tok[0:TOK, EXPERTS:2 * EXPERTS]
                    T.matmul(ranks, earlier[:], chosen[:, p.slot(2)].rearrange("p b e -> p (b e)"), start=True, stop=False)
                    T.matmul(second, ones_bf[0:TOK, :], chosen[:, p.slot(2), 0, :], start=False, stop=False)
                    for b in range(2):
                        last = T.matmul(ranks, ones_bf[:, :], so_far[:, p.slot(2), b:b + 1, :].to_broadcast([P, 2, EXPERTS]),
                                        start=False, stop=(b == 1))
                    last.then_inc(rank_done, 1)
                if (i - 3).within(PAIRS):
                    p = i - 3
                    pe.wait_ge(xn2_ready, p.upto())
                    if (p + 4).within(PAIRS):
                        pe.wait_ge(xnT_lo_ready, p.upto(-4))
                    else:
                        pe.wait_ge(xn2T_ready, p.upto(1))
                    for k in range(KC):
                        for b in range(2):
                            at = (2 * k + b) * TOK
                            last = T.transpose(b_turn[:, at:at + TOK], xn2[:, b, k * P:(k + 1) * P], ident[0:TOK, 0:TOK])
                    last.then_inc(turn2_done, 1)
                if i.within(PAIRS):
                    p = i
                    if p.had(2):
                        pe.wait_ge(h2_ready, p.upto(2))
                    elif p.had(1):
                        pe.wait_ge(q_parts, p.upto(1))
                    for c in range(KC):
                        for k in range(KC):
                            w = slice(c * P, (c + 1) * P)
                            last = product(b_qo[:, c * QW:(c + 1) * QW], (wq_hi[:, k, w], wq_lo[:, k, w]),
                                           (xnT_hi[:, p.slot(2), k, :], xnT_lo[:, p.slot(2), k, :]), k == 0, k == KC - 1)
                    last.then_inc(q_done, 1)
                if (i + 3).within(PAIRS):
                    p = i + 3
                    until, until2 = ahead(pe, p.upto()), ahead(pe, p.upto(7 if p.had(7) else 1))
                    pe.wait_ge(s_posb, 1)
                    pe.wait_ge(tokT_ready, until)
                    if p.had(7):
                        pe.wait_ge(place_ready, until2)
                    elif p.had(1):
                        pe.wait_ge(h_ready, until2)
                    for b in range(2):
                        for c in range(KC):
                            at = b * D + c * P
                            last = T.transpose(b_tok[0:PATCHES + 1, at:at + P], tokT[:, c, b, :], ident)
                    last.then_inc(back_done, 1)
                if (i - 3).within(PAIRS):
                    p = i - 3
                    pe.wait_ge(xn2T_ready, p.upto())
                    if (p + 1).within(PAIRS) and not is_last(p + 1):
                        pe.wait_ge(attnT_lo_ready, p.upto(-1))
                    else:
                        pe.wait_ge(ranked_ready, p.upto(1))
                    for b in range(2):
                        for k in range(KC):
                            last = T.matmul(b_gate[0:TOK, b * EXPERTS:(b + 1) * EXPERTS], xn2T[:, k, b * TOK:(b + 1) * TOK],
                                            gate_s[:, k, :], start=(k == 0), stop=(k == KC - 1))
                    last.then_inc(gate_done, 1)

            def early_step(n):
                pe.wait_ge(s_const, 16 * CONST_DMAS)
                pe.wait_ge(s_posb, 1)
                step(Turn(0, n))

            units(pe, unit, [0, 1, 2, 3, lambda: early_step(-3), "steady", 12, lambda: early_step(-2), 13, 14,
                             lambda: early_step(-1), 15])
            pe.wait_ge(s_posb, 2)
            pe.wait_ge(weight_step, 6)
            pe.wait_ge(s_bias_dma, 48)
            pe.wait_ge(patches_ready, IMAGES // OCT)
            walk(pe, BEFORE_A, STEADY_A, AFTER_A, step)

            pe.wait_ge(so_far_ready, PAIRS)
            for b in range(2):
                T.matmul(region_ends, ones_bf[:, 0:1], so_far[:, PAIRS % 2, b, :], start=(b == 0), stop=(b == 1))
            for b in range(2):
                last = T.matmul(region_end, so_far[:, PAIRS % 2, b, :], ones_bf[:, 0:1], start=(b == 0), stop=(b == 1))
            last.then_inc(table_pe, 1)
            pe.wait_ge(table_step, 4)
            T.matmul(tile_ends, tiles_f[:], con["c_tri"], start=True, stop=True).then_inc(table_pe, 1)
            pe.wait_ge(table_ready, 3)
            pe.wait_ge(gu_lo_ready, EXPERTS)
            pe.wait_ge(down_lo_ready, EXPERTS)
            expert_of = [pe.alloc_register(f"expert{k}") for k in range(UNROLL_B)]
            before = {}
            pe.reg_load(expert_of, slot_expert[0:1, 0:UNROLL_B])

            def expert(t, now):
                if t.slot(UNROLL_B) > now.slot(UNROLL_B):
                    return before[t.slot(UNROLL_B)]
                return pe.snap(expert_of[t.slot(UNROLL_B)], min_val=0, max_val=EXPERTS - 1)

            def tile_step(j):
                if j.slot(UNROLL_B) == 0 and j.had(UNROLL_B):
                    for k in (UNROLL_B - 2, UNROLL_B - 1):
                        before[k] = pe.snap(expert_of[k], min_val=0, max_val=EXPERTS - 1)
                    if j.within(TILES):
                        pe.reg_load(expert_of, slot_expert[0:1, bass.ds(j.n, UNROLL_B)])
                if j.within(TILES):
                    t = j
                    e = expert(t, j)
                    pe.wait_ge(xsT_lo_ready, t.upto())
                    for k in range(KC):
                        last = product(b_tile(b_gu, t, 2 * INNER), (xsT_hi[:, t.slot(4), k, :], xsT_lo[:, t.slot(4), k, :]),
                                       (wgu_hi[:, bass.ds(e, 1), k, :], wgu_lo[:, bass.ds(e, 1), k, :]), k == 0, k == KC - 1)
                    last.then_inc(gu_done, 1)
                if (j + 2).within(TILES):
                    t = j + 2
                    pe.wait_ge(xs_ready, t.upto())
                    for k in range(KC):
                        last = T.transpose(b_tile(b_x, t, P, k * P), xs[:, t.slot(4), k * P:(k + 1) * P], ident)
                    last.then_inc(turn_x_done, 1)
                if (j - 1).within(TILES):
                    t = j - 1
                    pe.wait_ge(act_ready, t.upto())
                    T.transpose(b_tile(b_a, t, P), act_u[:, t.slot(2)], ident).then_inc(turn_a_done, 1)
                if (j - 2).within(TILES):
                    t = j - 2
                    e = expert(t, j)
                    pe.wait_ge(actT_lo_ready, t.upto())
                    if t.had(2):
                        pe.wait_ge(result_ready, t.upto(2))
                    product(b_tile(b_y, t, D), (actT_hi[:, t.slot(2)], actT_lo[:, t.slot(2)]),
                            (wdown_hi[:, bass.ds(e, 1), :], wdown_lo[:, bass.ds(e, 1), :]), True, True).then_inc(down_done, 1)

            walk(pe, BEFORE_B, STEADY_B, AFTER_B, tile_step, UNROLL_B)


def constants():
    f = np.float32
    d, h = np.arange(P), np.arange(HPC)
    own = (d[:, None] // DH == h[None, :]).astype(f)
    e = np.arange(EXPERTS)
    t = np.arange(TILES)
    region = np.zeros((P, 2 * EXPERTS), f)
    region[TOK, 0:EXPERTS] = e * REGION
    tables = {
        "c_ident": np.eye(P, dtype=f),
        "c_earlier": np.triu(np.ones((TOK, TOK), f), 1),
        "c_mask": np.concatenate([np.repeat(own, DH, axis=1), own], axis=1),
        "c_weight8": np.tile((EXPERTS - e).astype(f), (TOK, 1)),
        "c_region": region,
        "c_regcol": (e * REGION).astype(f)[:, None],
        "c_tri": np.concatenate([np.triu(np.ones((EXPERTS, EXPERTS), f)), np.eye(EXPERTS, dtype=f)], axis=1),
        "c_slot": np.repeat(t, EXPERTS).astype(f)[None],
        "c_slotrow": (t * P).astype(f)[None],
    }
    packed, at = np.zeros((P, CONST_W), f), 0
    for name, (height, width) in CONSTS.items():
        packed[0:height, at:at + width] = tables[name]
        at += width
    return packed


def token_ids():
    at = np.concatenate([np.arange(1, PATCHES + 1), [0], np.arange(PATCHES + 1, TOK)])
    return (np.arange(IMAGES)[None, :] * TOK + at[:, None]).astype(np.int32)


def kernel(**inputs):
    import numpy as _np
    import concourse.bacc as _bacc
    from concourse import mybir as _mybir
    from concourse.bass_utils import run_bass_kernel_spmd as _run

    v = {k.replace("L0_", ""): _np.asarray(a) for k, a in inputs.items()}

    def chunks(a):
        return a.reshape(-1, P, a.shape[-1]).transpose(1, 0, 2)

    px = 16
    patches = v["x"].reshape(IMAGES // OCT, OCT, 3, 6, px, 6, px).transpose(0, 2, 4, 6, 1, 3, 5)
    layout = {
        "x": patches.reshape(IMAGES // OCT, 2, FC // 2, P, OCT * PATCHES).transpose(0, 1, 3, 2, 4)
             .reshape(2 * IMAGES // OCT, P, -1),
        "txt": v["txt"].transpose(1, 0, 2),
        "w_tok": chunks(v["tok_W"].T).reshape(P, -1),
        "pos": chunks(v["tok_pos_enc"][0].T),
        "tok_b": v["tok_b"].reshape(KC, P).T,
        "cls": v["tok_cls_token"].reshape(KC, P).T,
        "wq": chunks(v["attn_Wq"].T).reshape(P, -1),
        "bq": v["attn_bq"].reshape(KC, P).T,
        "wkv": chunks(_np.concatenate([v["attn_Wk"].T, v["attn_Wv"].T], axis=1)).reshape(P, -1),
        "bkv": _np.concatenate([v["attn_bk"], v["attn_bv"]])[None],
        "wo": chunks(v["attn_Wo"].T).reshape(P, -1),
        "bo": v["attn_bo"][None],
        "gate": chunks(v["ffn_gate_w"].T),
        "wgu": _np.concatenate([v["ffn_w_gate"], v["ffn_w_up"]], axis=1).transpose(2, 0, 1)
               .reshape(KC, P, EXPERTS, 2 * INNER).transpose(1, 2, 0, 3).reshape(P, -1),
        "wdown": v["ffn_w_down"].transpose(2, 0, 1).reshape(P, -1),
        "ids": token_ids(),
    }
    layout["consts"] = constants()
    nc = _bacc.Bacc("TRN2", target_bir_lowering=False, num_devices=1)
    arrays, args = {}, {}
    for name, a in layout.items():
        a = _np.ascontiguousarray(a)
        arrays[f"in_{name}"] = a
        args[name] = nc.dram_tensor(f"in_{name}", a.shape, _mybir.dt.from_np(a.dtype), kind="ExternalInput").ap()
    out = nc.dram_tensor("out_0", (TOKENS, D), _mybir.dt.float32, kind="ExternalOutput").ap()
    build(nc, out=out, **args)
    r = _run(nc, [arrays], core_ids=[0])
    return r.results[0]["out_0"].reshape(IMAGES, TOK, D)
```
